# Optimizing a Trainium2 kernel written in Bass

```python
import numpy as np
import jax
import jax.numpy as jnp

def _softmax(x, axis=-1):
    return jax.nn.softmax(x, axis=axis)

def _gelu(x):
    return jax.nn.gelu(x, approximate=True)

def _silu(x):
    return jax.nn.silu(x)

def _sigmoid(x):
    return jax.nn.sigmoid(x)

def _layernorm(x, axis=-1, eps=1e-05):
    m = jnp.mean(x, axis=axis, keepdims=True)
    v = jnp.var(x, axis=axis, keepdims=True)
    return (x - m) / jnp.sqrt(v + eps)

def _scatter_add(tgt, idx, src, axis=0):
    return tgt.at[idx].add(src)

def _segment_sum(src, seg, n):
    return jax.ops.segment_sum(src, seg, n)
kernel_name = 'mk_cond_seq_d1_seqx_r4_596338'

def setup_inputs(seed: int=0):
    np.random.seed(seed)
    _w = jnp.asarray

    def _rec_inputs():
        import jax
        import jax.numpy as jnp
        _rk = jax.random.key(seed)
        x = 7.22e-05 + 1 * jax.random.normal(jax.random.fold_in(_rk, 1), (4, 512, 256), jnp.float32)
        _lenS = 512 - jax.random.randint(jax.random.fold_in(_rk, 7), (4,), 0, max(1, 512 // 4) + 1, jnp.int32)
        _lenS2 = 512 - jax.random.randint(jax.random.fold_in(_rk, 8), (4,), 0, max(1, 512 // 4) + 1, jnp.int32)
        cond_1024 = 0.00782532 + 1.00527 * jax.random.normal(jax.random.fold_in(_rk, 11), (4, 256), jnp.float32)
        return (x, cond_1024)
    x, cond_1024 = _rec_inputs()

    def _L0_cond_setup():
        import jax, jax.numpy as jnp
        import numpy as np
        B, N, C = (8, 256, 256)
        H = 16
        D = C // H
        MLP = 4 * C
        EPS = 1e-06

        def _ln(x, w, b):
            m = jnp.mean(x, axis=-1, keepdims=True)
            v = jnp.mean(jnp.square(x - m), axis=-1, keepdims=True)
            return (x - m) * jax.lax.rsqrt(v + EPS) * w + b

        def _attention(x, gamma_qkv, gamma_attn_out, w_qkv, b_qkv, w_proj, b_proj):
            b, n, c = x.shape
            qkv = (x @ w_qkv + b_qkv) * gamma_qkv
            qkv = qkv.reshape(b, n, 3, H, D)
            q, k, v = (qkv[:, :, 0], qkv[:, :, 1], qkv[:, :, 2])
            scale = D ** (-0.5)
            attn = jnp.einsum('bqhd,bkhd->bhqk', q, k) * scale
            attn = jax.nn.softmax(attn, axis=-1)
            out = jnp.einsum('bhqk,bkhd->bqhd', attn, v).reshape(b, n, c)
            return gamma_attn_out * (out @ w_proj + b_proj)
        key = jax.random.key(seed)
        ks = jax.random.split(key, 12)
        s = 0.02
        return {'x': jax.random.normal(ks[0], (B, N, C), jnp.float32), 'c': jax.random.normal(ks[1], (B, C), jnp.float32), 'ln1_w': jnp.ones((C,), jnp.float32), 'ln1_b': jnp.zeros((C,), jnp.float32), 'ln2_w': jnp.ones((C,), jnp.float32), 'ln2_b': jnp.zeros((C,), jnp.float32), 'gamma_qkv': jnp.ones((3 * C,), jnp.float32), 'gamma_attn_out': jnp.ones((C,), jnp.float32), 'w_qkv': jax.random.normal(ks[2], (C, 3 * C), jnp.float32) * s, 'b_qkv': jnp.zeros((3 * C,), jnp.float32), 'w_proj': jax.random.normal(ks[3], (C, C), jnp.float32) * s, 'b_proj': jnp.zeros((C,), jnp.float32), 'w_fc1': jax.random.normal(ks[4], (C, MLP), jnp.float32) * s, 'b_fc1': jnp.zeros((MLP,), jnp.float32), 'w_fc2': jax.random.normal(ks[5], (MLP, C), jnp.float32) * s, 'b_fc2': jnp.zeros((C,), jnp.float32), 'w_ada': jax.random.normal(ks[6], (C, 6 * C), jnp.float32) * s, 'b_ada': jnp.zeros((6 * C,), jnp.float32), 'gamma1': jnp.ones((C,), jnp.float32), 'gamma2': jnp.ones((C,), jnp.float32)}
    _L0_cond_all = _L0_cond_setup()
    _L0_cond_in = {k: v for k, v in _L0_cond_all.items() if k in ('ln1_w', 'ln1_b', 'ln2_w', 'ln2_b', 'gamma_qkv', 'gamma_attn_out', 'w_qkv', 'b_qkv', 'w_proj', 'b_proj', 'w_fc1', 'b_fc1', 'w_fc2', 'b_fc2', 'w_ada', 'b_ada', 'gamma1', 'gamma2')}
    del _L0_cond_all
    return {'x': x, 'cond_1024': cond_1024, 'L0_cond_ln1_w': _L0_cond_in['ln1_w'], 'L0_cond_ln1_b': _L0_cond_in['ln1_b'], 'L0_cond_ln2_w': _L0_cond_in['ln2_w'], 'L0_cond_ln2_b': _L0_cond_in['ln2_b'], 'L0_cond_gamma_qkv': _L0_cond_in['gamma_qkv'], 'L0_cond_gamma_attn_out': _L0_cond_in['gamma_attn_out'], 'L0_cond_w_qkv': _L0_cond_in['w_qkv'], 'L0_cond_b_qkv': _L0_cond_in['b_qkv'], 'L0_cond_w_proj': _L0_cond_in['w_proj'], 'L0_cond_b_proj': _L0_cond_in['b_proj'], 'L0_cond_w_fc1': _L0_cond_in['w_fc1'], 'L0_cond_b_fc1': _L0_cond_in['b_fc1'], 'L0_cond_w_fc2': _L0_cond_in['w_fc2'], 'L0_cond_b_fc2': _L0_cond_in['b_fc2'], 'L0_cond_w_ada': _L0_cond_in['w_ada'], 'L0_cond_b_ada': _L0_cond_in['b_ada'], 'L0_cond_gamma1': _L0_cond_in['gamma1'], 'L0_cond_gamma2': _L0_cond_in['gamma2']}

def reference(x, cond_1024, L0_cond_ln1_w, L0_cond_ln1_b, L0_cond_ln2_w, L0_cond_ln2_b, L0_cond_gamma_qkv, L0_cond_gamma_attn_out, L0_cond_w_qkv, L0_cond_b_qkv, L0_cond_w_proj, L0_cond_b_proj, L0_cond_w_fc1, L0_cond_b_fc1, L0_cond_w_fc2, L0_cond_b_fc2, L0_cond_w_ada, L0_cond_b_ada, L0_cond_gamma1, L0_cond_gamma2):
    import jax
    import jax.numpy as jnp

    def _L0_cond_ref(x, c, ln1_w, ln1_b, ln2_w, ln2_b, gamma_qkv, gamma_attn_out, w_qkv, b_qkv, w_proj, b_proj, w_fc1, b_fc1, w_fc2, b_fc2, w_ada, b_ada, gamma1, gamma2):
        import jax, jax.numpy as jnp
        import numpy as np
        B, N, C = (8, 256, 256)
        H = 16
        D = C // H
        MLP = 4 * C
        EPS = 1e-06

        def _ln(x, w, b):
            m = jnp.mean(x, axis=-1, keepdims=True)
            v = jnp.mean(jnp.square(x - m), axis=-1, keepdims=True)
            return (x - m) * jax.lax.rsqrt(v + EPS) * w + b

        def _attention(x, gamma_qkv, gamma_attn_out, w_qkv, b_qkv, w_proj, b_proj):
            b, n, c = x.shape
            qkv = (x @ w_qkv + b_qkv) * gamma_qkv
            qkv = qkv.reshape(b, n, 3, H, D)
            q, k, v = (qkv[:, :, 0], qkv[:, :, 1], qkv[:, :, 2])
            scale = D ** (-0.5)
            attn = jnp.einsum('bqhd,bkhd->bhqk', q, k) * scale
            attn = jax.nn.softmax(attn, axis=-1)
            out = jnp.einsum('bhqk,bkhd->bqhd', attn, v).reshape(b, n, c)
            return gamma_attn_out * (out @ w_proj + b_proj)
        ada = jax.nn.silu(c) @ w_ada + b_ada
        sh_msa, sc_msa, g_msa, sh_mlp, sc_mlp, g_mlp = [a[:, None, :] for a in jnp.split(ada, 6, axis=-1)]
        h = _ln(x, ln1_w, ln1_b) * (1 + sc_msa) + sh_msa
        x = x + gamma1 * g_msa * _attention(h, gamma_qkv, gamma_attn_out, w_qkv, b_qkv, w_proj, b_proj)
        h = _ln(x, ln2_w, ln2_b) * (1 + sc_mlp) + sh_mlp
        mlp = jax.nn.gelu(h @ w_fc1 + b_fc1, approximate=True) @ w_fc2 + b_fc2
        x = x + gamma2 * g_mlp * mlp
        return x
    x = _L0_cond_ref(x, cond_1024, L0_cond_ln1_w, L0_cond_ln1_b, L0_cond_ln2_w, L0_cond_ln2_b, L0_cond_gamma_qkv, L0_cond_gamma_attn_out, L0_cond_w_qkv, L0_cond_b_qkv, L0_cond_w_proj, L0_cond_b_proj, L0_cond_w_fc1, L0_cond_b_fc1, L0_cond_w_fc2, L0_cond_b_fc2, L0_cond_w_ada, L0_cond_b_ada, L0_cond_gamma1, L0_cond_gamma2)
    return x

_drawn_inputs = setup_inputs


def setup_inputs(seed=0):
    import zlib

    import numpy as np

    out = dict(_drawn_inputs(seed))
    spreads = {'L0_cond_ln1_w': (1.0, 0.6),
     'L0_cond_ln1_b': (0.0, 0.8),
     'L0_cond_ln2_w': (1.0, 0.6),
     'L0_cond_ln2_b': (0.0, 2.0),
     'L0_cond_gamma_qkv': (1.0, 0.6),
     'L0_cond_gamma_attn_out': (1.0, 0.6),
     'L0_cond_b_qkv': (0.0, 0.8),
     'L0_cond_b_proj': (0.0, 0.951),
     'L0_cond_b_fc1': (0.0, 2.0),
     'L0_cond_b_fc2': (0.0, 1.409),
     'L0_cond_b_ada': (0.0, 0.359),
     'L0_cond_gamma1': (1.0, 0.6),
     'L0_cond_gamma2': (1.0, 0.6)}
    factors = {'L0_cond_w_qkv': 8.0, 'L0_cond_w_proj': 5.739, 'L0_cond_w_fc1': 3.559}
    for name, (base, spread) in spreads.items():
        noise = np.random.default_rng([zlib.crc32(name.encode()), seed]).standard_normal(out[name].shape)
        drawn = base * np.exp(spread * noise) if base else spread * noise
        out[name] = jnp.asarray(drawn.astype(out[name].dtype))
    for name, factor in factors.items():
        out[name] = (out[name] * factor).astype(out[name].dtype)
    return out
```

```python
from contextlib import ExitStack

import concourse.bass as bass
from concourse import mybir

F32 = mybir.dt.float32
F32R = mybir.dt.float32r
I32 = mybir.dt.int32
ALU = mybir.AluOpType
ACT = mybir.ActivationFunctionType
AX = mybir.AxisListType

P = 128
B, N, C, H = 4, 512, 256, 16
D = C // H
MLP = 4 * C
KT = C // P
TT = N // P
NT = B * TT
G = 4
GH = H // G
FN = MLP // P
HALF = N // 2
STEPS = B * G * TT
RING = 3
EPS = 1e-6
GELU_CUBIC = 0.044715
GELU_SCALE = 0.7978845608028654
RSQRT_SEED = 1597463007.0
QROWS, MROWS = 3 * D, 2

COLS = {}
for _name, _n in (("qk_b", 4), ("qk_g", 4), ("ln1_w", 2), ("ln1_b", 2), ("ln2_w", 2), ("ln2_b", 2),
                  ("fc1_b", FN), ("ada_b", 12), ("cond", 2 * B)):
    COLS[_name] = (sum(n for _, n in COLS.values()), _n)
NCOLS = sum(n for _, n in COLS.values())
ROW_BV, ROW_GV, ROW_BP, ROW_B2 = range(4)
TROW_G1, TROW_GO, TROW_G2, TROW_AMSA, TROW_AMLP = range(5)
SH_MSA, SC_MSA, G_MSA, SH_MLP, SC_MLP, G_MLP = range(6)


def make_plan():
    plan, fills, used = [], [], {"act": 0, "dve": 0}
    uses = {"split": 0, "gelu": 0}

    def do(kind, *args):
        plan.append((kind, args))

    def fill(kind, *args):
        eng = "act" if kind in ("turn1", "turn2", "qk", "maxrow", "fc1") else "dve"
        used[eng] += 1
        f = {"kind": kind, "args": args, "n": len(fills), "slot": len(fills) % RING,
             "eng": eng, "count": used[eng]}
        if kind in ("turn1", "turn2", "qk"):
            f["split"] = uses["split"]
            uses["split"] += 1
        if kind == "fc1":
            f["gelu"] = uses["gelu"]
            uses["gelu"] += 1
        fills.append(f)
        plan.append(("fill", (f,)))
        return f

    def maxes(n):
        b, g = divmod(n, G)
        return [("max", b, g, j, t) for t in range(TT) for j in range(GH)]

    do("setup")
    fill("ada", 0)
    do("ln1", 0)
    for k in range(KT):
        fill("turn1", 0, k)
    fill("qk", 0, 0, 0)
    fill("qk", 0, 1, 0)
    do("qk_rows", 0, 0)
    for t in range(TT):
        fill("v", 0, t)
    do("v_place", 0)
    fill("qk", 0, 0, 1)
    fill("qk", 0, 1, 1)
    do("qk_rows", 0, 1)
    for m in maxes(0):
        fill(*m)
    fill("maxrow", 0, 0)
    do("ln1", 1)

    for s in range(STEPS):
        b, i = divmod(s, G * TT)
        n, kt = divmod(s, TT)
        own, after = [], []
        nxt = maxes(n + 1) if n + 1 < B * G else []
        lot = nxt[(0, 6, 11, 16)[kt]:(6, 11, 16, 16)[kt]]
        if kt == 3 and nxt:
            own.append(("maxrow",) + divmod(n + 1, G))
        nb, pb = b + 1, b - 1
        if nb < B:
            if i == 0:
                own += [("turn1", nb, 0), ("turn1", nb, 1)]
            if i == 2:
                own += [("qk", nb, 0, 0), ("qk", nb, 1, 0)]
            if i in (4, 5):
                own += [("v", nb, 2 * (i - 4)), ("v", nb, 2 * (i - 4) + 1)]
            if i == 11:
                own += [("qk", nb, 0, 1), ("qk", nb, 1, 1)]
            if i == 6:
                after.append(("residual1", nb))
            if i == 7:
                after.append(("qk_rows", nb, 0))
            if i == 13 and nb + 1 < B:
                after.append(("ln1", nb + 1))
        if b == 0:
            if i < 4:
                own += [("gate", i, 0), ("gate", i, 1)]
            if i == 4:
                own.append(("ada", 1))
                after.append(("residual1", 0))
            if i in (5, 6, 7, 8, 9):
                after.append(("weights", i - 5))
        if pb >= 0:
            if i == 3:
                own += [("proj", pb, t) for t in range(TT)]
                after.append(("ln2", pb))
            if i == 6:
                own += [("turn2", pb, 0), ("turn2", pb, 1)]
                after.append(("residual2", pb))
            if i in (7, 8):
                own += [("fc1", pb, 0, 2 * (i - 7)), ("fc1", pb, 0, 2 * (i - 7) + 1)]
            if i in (9, 10):
                own += [("fc2", pb, i - 9)]
            if i in (11, 12):
                own += [("fc1", pb, 1, 2 * (i - 11)), ("fc1", pb, 1, 2 * (i - 11) + 1)]
            if i in (14, 15):
                own += [("fc2", pb, i - 12)]
        mixed, lot = [], list(lot)
        every = max(1, -(-len(lot) // (len(own) + 1)))
        while lot or own:
            mixed += lot[:every]
            lot = lot[every:]
            if own:
                mixed.append(own.pop(0))
        cut = [0, len(mixed) // 3, 2 * len(mixed) // 3, len(mixed)]
        late = []

        def put(lo, hi):
            for m in mixed[lo:hi]:
                for x in late:
                    do(*x.pop(0))
                late[:] = [x for x in late if x]
                f = fill(*m)
                if m[0] == "fc1":
                    late.append([("gelu_b", f), ("gelu_c", f), ("gelu_d", f)])

        do("scores", s, 0)
        put(cut[0], cut[1])
        do("scores", s, 1)
        put(cut[1], cut[2])
        if s >= 1:
            do("values", s - 1)
            if i == 0:
                do("v_place", b)
            if s % TT == 0:
                do("attn_out", n - 1)
        put(cut[2], cut[3])
        while late:
            for x in late:
                do(*x.pop(0))
            late = [x for x in late if x]
        if i == 0 and b >= 1:
            do("normalise", b - 1)
            do("qk_rows", b, 1)
        for x in after:
            do(*x)

    last = B - 1
    do("values", STEPS - 1)
    do("attn_out", B * G - 1)
    do("normalise", last)
    for t in range(TT):
        fill("proj", last, t)
    do("ln2", last)
    fill("turn2", last, 0)
    fill("turn2", last, 1)
    do("residual2", last)
    for half in range(2):
        lots = [fill("fc1", last, half, 0)]
        for k in range(1, 4):
            do("gelu_b", lots[-1])
            lots.append(fill("fc1", last, half, k))
            do("gelu_c", lots[-2])
            do("gelu_d", lots[-2])
        do("gelu_b", lots[-1])
        do("gelu_c", lots[-1])
        do("gelu_d", lots[-1])
        for t in range(2):
            fill("fc2", last, 2 * half + t)
    return plan, fills


def block_program(nc, x, cols, rows, trows, w_qkv, w_proj, w_fc1, w_fc2, w_ada, out):
    plan, fills = make_plan()

    def find(kind, *args):
        for f in fills:
            if f["kind"] == kind and f["args"] == args:
                return f
        raise KeyError((kind, args))

    with ExitStack() as ctx:
        def sb(name, shape, dt=F32):
            return ctx.enter_context(nc.sbuf_tensor(name, shape, dt))

        def sem(name):
            return ctx.enter_context(nc.semaphore(name))

        X = sb("X", [P, NT, C])
        wqkv_h, wqkv_l = sb("wqkv_h", [P, KT, 3 * C], F32R), sb("wqkv_l", [P, KT, 3 * C], F32R)
        wp_h, wp_l = sb("wp_h", [P, KT, C], F32R), sb("wp_l", [P, KT, C], F32R)
        w1_h, w1_l = sb("w1_h", [P, KT, MLP], F32R), sb("w1_l", [P, KT, MLP], F32R)
        w2_h, w2_l = sb("w2_h", [P, FN, C], F32R), sb("w2_l", [P, FN, C], F32R)
        QA = sb("QA", [P, H // 2, N], F32R)
        KA = sb("KA", [P, H // 2, N], F32R)
        QK = sb("QK", [P, 2, 2, N], F32R)
        PB = sb("PB", [P, 2, GH, N])
        VA = sb("VA", [P, TT, H, 2 * D])
        HT = sb("HT", [P, 2, KT, N], F32R)
        AH = sb("AH", [P, 2, KT, N], F32R)
        FULL = sb("FULL", [P, 2, N])
        NRM = sb("NRM", [P, TT, C])
        OS = sb("OS", [P, N])
        OC = sb("OC", [P, KT, N])
        LC = sb("LC", [P, KT, N])
        RW = sb("RW", [P, 4, C])
        GATE = sb("GATE", [P, B, 2, C])
        GB = sb("GB", [P, C])
        XV = sb("XV", [P, 2, 2, 2, HALF])
        XG, VG = XV[:, 0, :, :, :], XV[:, 1, :, :, :]
        XV_flat = XV[:, :, :, :, :].rearrange("p a q e n -> p (a q e n)")
        TR = XV_flat[:, 0:5 * C].rearrange("p (r c) -> p r c", r=5)
        w_praw = XV_flat[:, 5 * C:7 * C].rearrange("p (k c) -> p k c", k=KT)
        VT = sb("VT", [P, TT, C])
        PT = sb("PT", [P, C])
        ident = sb("ident", [P, P])
        MR = sb("MR", [2 * GH, N], F32R)
        nm = sb("nm", [P, TT, GH])
        ms = sb("ms", [P, TT, 2 * GH], F32R)
        PC = sb("PC", [P, NCOLS])
        qkb = sb("qkb", [P, 4])
        qkg = sb("qkg", [P, 4])
        adab1 = sb("adab1", [P, 12])
        silu = sb("silu", [P, 2 * B])
        tnh = sb("tnh", [P, 2 * B])
        LA = sb("LA", [P, 2, KT, B])
        LB = sb("LB", [P, 2, KT, B])
        lt = sb("lt", [P, KT, B])
        st6 = sb("st6", [P, TT, 6])
        mv = sb("mv", [P, TT, 2])
        ve = sb("ve", [P, TT])
        rs = sb("rs", [P, TT])
        rt = sb("rt", [P, TT])
        nmr = sb("nmr", [P, TT])
        with nc.sbuf_tensor("w_adaraw", [P, KT, 6 * C], F32) as w_adaraw:
            pass
        with nc.sbuf_tensor("w_1raw", [P, KT, MLP], F32) as w_1raw, \
                nc.sbuf_tensor("w_2raw", [P, FN, C], F32) as w_2raw:
            pass
        U = sb("U", [P, 2, FN, HALF], F32R)
        silu_wide = OC[:, :, :].rearrange("p k n -> p (k n)").rearrange("p (k b m) -> p k b m", k=KT, b=B)
        w_qraw = PB[:, 1, :, :].rearrange("p j n -> p (j n)")[:, 0:KT * 3 * C].rearrange("p (k n) -> p k n", k=KT)

        ST = [ctx.enter_context(nc.psum_tensor(f"ST{i}", [P, 2, N], F32)) for i in range(2)]
        SM = [ctx.enter_context(nc.psum_tensor(f"SM{i}", [P, N], F32)) for i in range(RING)]
        O = ctx.enter_context(nc.psum_tensor("O", [P, N], F32))

        cols_in, rows_in, trows_in, ada0_in, ada1_in = map(sem, ("cols_in", "rows_in", "trows_in", "ada0_in", "ada1_in"))
        wq_in, wp_in, w1_in, w2_in, ones_in = map(sem, ("wq_in", "wp_in", "w1_in", "w2_in", "ones_in"))
        x_in = [sem(f"x_in{b}") for b in range(B)]
        consts = sem("consts")
        pool_seq = sem("pool_seq")
        tanh_c = sem("tanh_c")
        dve_seq = sem("dve_seq")
        silu_ready = sem("silu_ready")
        wq_hi, wq_split = sem("wq_hi"), sem("wq_split")
        w_split = sem("w_split")
        filled = sem("filled")
        rel = {"act": sem("act_took"), "dve": sem("dve_took")}
        affine = sem("affine")
        stats = sem("stats")
        normed = sem("normed")
        split = sem("split")
        qk_in = [sem("qk_in0"), sem("qk_in1")]
        mrow_in = [sem("mrow_in0"), sem("mrow_in1")]
        maxed = sem("maxed")
        v_biased, v_ready = sem("v_biased"), sem("v_ready")
        scored, exped, valued = sem("scored"), sem("exped"), sem("valued")
        o_copied, o_in = sem("o_copied"), sem("o_in")
        recip, attn_full, attn_hi, attn_split = map(sem, ("recip", "attn_full", "attn_hi", "attn_split"))
        gate_raw, gate_ready = sem("gate_raw"), sem("gate_ready")
        res1, res2 = sem("res1"), sem("res2")
        x2_ready = sem("x2_ready")
        g_mid, g_tanh, g_full, u_ready = map(sem, ("g_mid", "g_tanh", "g_full", "u_ready"))
        y_ready, y_out = sem("y_ready"), sem("y_out")

        def col(name, i, n=1):
            return PC[:, COLS[name][0] + i:COLS[name][0] + i + n]

        def half_rows(h):
            return 64 * (h % 2)

        ln_order = [(k, a[0]) for k, a in plan if k in ("ln1", "ln2")]
        res_order = [(k, a[0]) for k, a in plan if k in ("residual1", "residual2")]
        block = ctx.enter_context(nc.Block())

        @block.sync
        def _(sp):
            for kind, a in plan:
                if kind == "setup":
                    sp.dma_start(PC[:, :], cols).then_inc(cols_in, 16)
                    xv = x.rearrange("b (t p) c -> b p t c", p=P)
                    av = w_ada.rearrange("(k p) n -> p k n", p=P)
                    sp.dma_start(X[:, 0:TT, :], xv[0]).then_inc(x_in[0], 16)
                    sp.dma_start(w_adaraw[:, :, 0:2 * C], av[:, :, 0:2 * C]).then_inc(ada0_in, 16)
                    sp.dma_start(w_qraw, w_qkv.rearrange("(k p) n -> p k n", p=P)).then_inc(wq_in, 16)
                    sp.dma_start(RW[:, :, :].rearrange("p r c -> p (r c)"),
                                 rows.broadcast_to([P, 4 * C])).then_inc(rows_in, 16)
                    sp.wait_ge(consts, 3)
                    for half in range(2):
                        for j in range(H // 2):
                            sp.dma_start(KA[64 * half + QROWS:64 * half + QROWS + MROWS, j, :].bitcast(F32),
                                         MR[0:MROWS, :].bitcast(F32)).then_inc(ones_in, 16)
                    sp.dma_start(w_adaraw[:, :, 2 * C:6 * C], av[:, :, 2 * C:6 * C]).then_inc(ada1_in, 16)
                    sp.dma_start(TR[:, :, :].rearrange("p r c -> p (r c)"),
                                 trows.broadcast_to([P, 5 * C])).then_inc(trows_in, 16)
                    for b in range(1, B):
                        sp.dma_start(X[:, b * TT:(b + 1) * TT, :], xv[b]).then_inc(x_in[b], 16)
                    sp.dma_start(w_praw[:, :, :], w_proj.rearrange("(k p) n -> p k n", p=P)).then_inc(wp_in, 16)
                if kind == "fill" and a[0]["kind"] == "ada" and a[0]["args"] == (1,):
                    sp.wait_ge(filled, a[0]["n"] + 1)
                    sp.wait_ge(gate_ready, 2 * B)
                    sp.dma_start(w_1raw[:, :, :], w_fc1.rearrange("(k p) n -> p k n", p=P)).then_inc(w1_in, 16)
                    sp.dma_start(w_2raw[:, :, :], w_fc2.rearrange("(k p) n -> p k n", p=P)).then_inc(w2_in, 16)
                if kind == "qk_rows":
                    b, mt = a
                    sp.wait_ge(split, find("qk", b, 1, mt)["split"] + 1)
                    if b >= 1:
                        sp.wait_ge(scored, 2 * ((b - 1) * G * TT + (8 if mt == 0 else 16)))
                    for half in range(2):
                        for dst, which, parts in ((QA, 0, (0, 0, 1)), (KA, 1, (0, 1, 0))):
                            for blk, hl in enumerate(parts):
                                sp.dma_start(
                                    dst[64 * half + D * blk:64 * half + D * (blk + 1), 4 * mt:4 * mt + 4, :].bitcast(F32),
                                    QK[64 * half:64 * half + 64, which, hl, :].bitcast(F32)).then_inc(qk_in[mt], 16)
                if kind == "fill" and a[0]["kind"] == "maxrow":
                    b, g = a[0]["args"]
                    sp.wait_ge(rel["act"], a[0]["count"])
                    for half in range(2):
                        sp.dma_start(QA[64 * half + QROWS:64 * half + QROWS + MROWS, 2 * g:2 * g + 2, :].bitcast(F32),
                                     MR[4 * half:4 * half + 4, :].bitcast(F32)).then_inc(mrow_in[g % 2], 16)
                if kind == "attn_out":
                    n = a[0]
                    b, g = divmod(n, G)
                    sp.wait_ge(o_copied, n + 1)
                    if n == 0:
                        sp.wait_ge(filled, find("gate", B - 1, 1)["n"] + 1)
                    if g == 0 and b >= 1:
                        sp.wait_ge(attn_split, b)
                        sp.wait_ge(attn_full, b)
                    part = slice(64 * (g % 2), 64 * (g % 2) + 64)
                    sp.dma_start(OC[part, g // 2, :], OS[0:P:2, :]).then_inc(o_in, 16)
                    sp.dma_start(LC[part, g // 2, :], OS[1:P:2, :]).then_inc(o_in, 16)
                if kind == "fill" and a[0]["kind"] == "fc2":
                    b, t = a[0]["args"]
                    k = b * TT + t
                    sp.wait_ge(y_ready, k + 1)
                    sp.dma_start(out[b, t * P:(t + 1) * P, :], X[:, k, :]).then_inc(y_out, 16)
            sp.wait_ge(y_out, 16 * NT)

        @block.tensor
        def _(pe):
            def products(psum, left, right, tiles):
                parts = ((0, 0), (1, 0), (0, 1))
                for k in range(tiles):
                    for i, (l, r) in enumerate(parts):
                        mm = pe.matmul(psum, left(l, k), right(r, k), start=(k == 0 and i == 0),
                                       stop=(k == tiles - 1 and i == 2))
                return mm

            for kind, a in plan:
                if kind == "fill":
                    f = a[0]
                    if f["n"] >= RING:
                        old = fills[f["n"] - RING]
                        pe.wait_ge(rel[old["eng"]], old["count"])
                    ps = SM[f["slot"]]
                    what, args = f["kind"], f["args"]
                    if what == "ada":
                        pe.wait_ge(silu_ready, 1)
                        pe.wait_ge((ada0_in, ada1_in)[args[0]], 16)
                        first = SH_MLP if args[0] else SH_MSA
                        for c in range(2 * KT):
                            for k in range(KT):
                                mm = pe.matmul(ps[:, B * c:B * c + B],
                                               w_adaraw[:, k, first * C + c * P:first * C + (c + 1) * P],
                                               silu[:, k * B:(k + 1) * B], start=(k == 0), stop=(k == KT - 1))
                    elif what == "gate":
                        b, m = args
                        pe.wait_ge(silu_ready, 2)
                        pe.wait_ge(ada1_in, 16)
                        c0 = (G_MLP if m else G_MSA) * C
                        for k in range(KT):
                            mm = pe.matmul(ps[:, 0:C], silu_wide[:, k, b, :], w_adaraw[:, k, c0:c0 + C],
                                           start=(k == 0), stop=(k == KT - 1))
                    elif what in ("turn1", "turn2"):
                        b, k = args
                        pe.wait_ge(consts, 2)
                        pe.wait_ge(normed, ln_order.index(("ln" + what[-1], b)) + 1)
                        for t in range(TT):
                            mm = pe.transpose(ps[:, t * P:(t + 1) * P], NRM[:, t, k * P:(k + 1) * P], ident[:, :])
                    elif what == "qk":
                        b, which, mt = args
                        pe.wait_ge(wq_split, 1)
                        pe.wait_ge(split, find("turn1", b, KT - 1)["split"] + 1)
                        c0 = which * C + mt * P
                        mm = products(ps[:, :], lambda l, k: (wqkv_h, wqkv_l)[l][:, k, c0:c0 + P],
                                      lambda r, k: HT[:, r, k, :], KT)
                    elif what == "v":
                        b, t = args
                        mm = products(ps[:, 0:C], lambda l, k: HT[:, l, k, t * P:(t + 1) * P],
                                      lambda r, k: (wqkv_h, wqkv_l)[r][:, k, 2 * C:3 * C], KT)
                    elif what == "max":
                        b, g, j, t = args
                        h = g * GH + j
                        if (g % 2, j, t) == (0, 0, 0):
                            pe.wait_ge(qk_in[g // 2], 16 * 12 * (b + 1))
                        r = half_rows(h)
                        mm = pe.matmul(ps[:, :], QA[r:r + QROWS, h // 2, t * P:(t + 1) * P],
                                       KA[r:r + QROWS, h // 2, :], start=True, stop=True)
                    elif what == "maxrow":
                        b, g = args
                        pe.wait_ge(maxed, b * G + g + 1)
                        for t in range(TT):
                            mm = pe.transpose(ps[0:2 * GH, t * P:(t + 1) * P], ms[:, t, :].bitcast(F32), ident[:, :])
                    elif what == "proj":
                        b, t = args
                        pe.wait_ge(attn_split, b + 1)
                        pe.wait_ge(w_split, 1)
                        mm = products(ps[:, 0:C], lambda l, k: AH[:, l, k, t * P:(t + 1) * P],
                                      lambda r, k: (wp_h, wp_l)[r][:, k, :], KT)
                    elif what == "fc1":
                        b, half, i = args
                        pe.wait_ge(split, find("turn2", b, KT - 1)["split"] + 1)
                        pe.wait_ge(w_split, 3)
                        for e in range(2):
                            c0 = (2 * i + e) * P
                            mm = products(ps[:, e * HALF:(e + 1) * HALF], lambda l, k: (w1_h, w1_l)[l][:, k, c0:c0 + P],
                                          lambda r, k: AH[:, r, k, half * HALF:(half + 1) * HALF], KT)
                    elif what == "fc2":
                        b, t = args
                        pe.wait_ge(w_split, 5)
                        pe.wait_ge(u_ready, (2 * b + t // 2 + 1) * FN // 2)
                        c0 = (t % 2) * P
                        mm = products(ps[:, 0:C], lambda l, k: U[:, l, k, c0:c0 + P],
                                      lambda r, k: (w2_h, w2_l)[r][:, k, :], FN)
                    mm.then_inc(filled, 1)
                if kind == "scores":
                    s, half = a
                    b, i = divmod(s, G * TT)
                    g, kt = divmod(i, TT)
                    n = s // TT
                    if s >= 1:
                        pe.wait_ge(exped, 2 * (s - 1) + half + 1)
                    if kt == 0 and half == 0:
                        pe.wait_ge(mrow_in[g % 2], 32 * (n // 2 + 1))
                        if n == 0:
                            pe.wait_ge(ones_in, 16 * H)
                    for e in range(2):
                        h = g * GH + 2 * half + e
                        r = half_rows(h)
                        mm = pe.matmul(ST[half][:, e, :], KA[r:r + QROWS + MROWS, h // 2, kt * P:(kt + 1) * P],
                                       QA[r:r + QROWS + MROWS, h // 2, :], start=True, stop=True)
                    mm.then_inc(scored, 1)
                if kind == "values":
                    s = a[0]
                    b, i = divmod(s, G * TT)
                    g, kt = divmod(i, TT)
                    n = s // TT
                    pe.wait_ge(exped, 2 * s + 2)
                    if i == 0:
                        pe.wait_ge(v_ready, TT * (b + 1))
                    if kt == 0 and n >= 1:
                        pe.wait_ge(o_copied, n)
                    for j in range(GH):
                        mm = pe.matmul(O[2 * D * j:2 * D * (j + 1), :], VA[:, kt, g * GH + j, :],
                                       PB[:, s % 2, j, :], start=(kt == 0), stop=(kt == TT - 1))
                    mm.then_inc(valued, 1)

        @block.scalar
        def _(act):
            for kind, a in plan:
                if kind == "setup":
                    act.wait_ge(cols_in, 16)
                    act.activation(tnh[:, :], col("cond", 0, 2 * B), ACT.Tanh, scale=0.5).then_inc(tanh_c, 1)
                    act.wait_ge(wq_in, 16)
                    act.activation(wqkv_h[:, :, :], w_qraw, ACT.Copy).then_inc(wq_hi, 1)
                if kind == "fill" and a[0]["eng"] == "act":
                    f = a[0]
                    what, args, ps = f["kind"], f["args"], SM[f["slot"]]
                    act.wait_ge(filled, f["n"] + 1)
                    if what in ("turn1", "turn2", "qk"):
                        if f["split"] >= 2:
                            act.wait_ge(split, f["split"] - 1)
                        if what == "qk":
                            b, which, mt = args
                            if mt == 1:
                                act.wait_ge(qk_in[0], 16 * 12 * (b + 1))
                            elif b >= 1:
                                act.wait_ge(qk_in[1], 16 * 12 * b)
                            act.wait_ge(silu_ready, 1)
                            i = 2 * which + mt
                            dst, bias, scale = QK[:, which, 0, :], qkb[:, i:i + 1], qkg[:, i:i + 1]
                        else:
                            b, k = args
                            m = int(what[-1]) - 1
                            act.wait_ge(affine, m + 1)
                            dst = (HT, AH)[m][:, 0, k, :]
                            bias, scale = LB[:, m, k, b:b + 1], LA[:, m, k, b:b + 1]
                        act.activation(FULL[:, f["split"] % 2, :], ps[:, :], ACT.Identity, bias=bias, scale=scale)
                        act.activation(dst, ps[:, :], ACT.Identity, bias=bias, scale=scale).then_inc(rel["act"], 1)
                    elif what == "maxrow":
                        b, g = args
                        n = b * G + g
                        if n >= 1:
                            act.wait_ge(mrow_in[(g - 1) % 2], 32 * ((n - 1) // 2 + 1))
                        else:
                            act.wait_ge(ones_in, 16 * H)
                        act.activation(MR[:, :], ps[0:2 * GH, :], ACT.Copy).then_inc(rel["act"], 1)
                    elif what == "fc1":
                        b, half, i = args
                        q = f["gelu"]
                        if q >= 2:
                            act.wait_ge(u_ready, q - 1)
                        for func, dst in ((ACT.Identity, XG), (ACT.Square, VG)):
                            for e in range(2):
                                mm = act.activation(dst[:, q % 2, e, :], ps[:, e * HALF:(e + 1) * HALF], func,
                                                    bias=col("fc1_b", 2 * i + e))
                        mm.then_inc(rel["act"], 1)
                if kind == "gelu_c":
                    q = a[0]["gelu"]
                    act.wait_ge(g_mid, q + 1)
                    act.activation(VG[:, q % 2, :, :], VG[:, q % 2, :, :], ACT.Tanh,
                                   scale=GELU_SCALE * GELU_CUBIC).then_inc(g_tanh, 1)
                if kind == "scores":
                    s, half = a
                    act.wait_ge(scored, 2 * s + half + 1)
                    if s == 1:
                        act.wait_ge(wq_split, 1)
                    if s >= 2:
                        act.wait_ge(valued, s - 1)
                    act.activation(PB[:, s % 2, 2 * half:2 * half + 2, :], ST[half][:, :, :],
                                   ACT.Exp).then_inc(exped, 1)
                if kind == "attn_out":
                    n = a[0]
                    act.wait_ge(valued, TT * (n + 1))
                    if n >= 1:
                        act.wait_ge(o_in, 32 * n)
                    act.activation(OS[:, :], O[:, :], ACT.Copy).then_inc(o_copied, 1)
                if kind == "normalise":
                    b = a[0]
                    act.wait_ge(attn_full, b + 1)
                    if b >= 1:
                        act.wait_ge(filled, find("fc1", b - 1, 1, 3)["n"] + 1)
                    act.activation(AH[:, 0, :, :], OC[:, :, :], ACT.Copy).then_inc(attn_hi, 1)

        @block.vector
        def _(dve):
            done = [0]

            def link(ins):
                done[0] += 1
                ins.then_inc(dve_seq, 1)
                dve.wait_ge(dve_seq, done[0])

            def take(f):
                dve.wait_ge(filled, f["n"] + 1)
                return SM[f["slot"]]

            for kind, a in plan:
                if kind == "setup":
                    dve.wait_ge(cols_in, 16)
                    dve.wait_ge(tanh_c, 1)
                    link(dve.scalar_tensor_tensor(out=silu[:, :], in0=tnh[:, :], scalar=1.0,
                                                  in1=col("cond", 0, 2 * B), op0=ALU.add, op1=ALU.mult))
                    dve.tensor_scalar(qkg[:, 0:2], col("qk_g", 0, 2), float(D) ** -0.5, None, ALU.mult)
                    dve.tensor_copy(qkg[:, 2:4], col("qk_g", 2, 2))
                    dve.tensor_scalar(adab1[:, :], col("ada_b", 0, 12), 1.0, None, ALU.add)
                    link(dve.tensor_scalar(silu[:, :], silu[:, :], 0.5, None, ALU.mult))
                    dve.tensor_tensor(qkb[:, :], col("qk_b", 0, 4), qkg[:, :], ALU.mult).then_inc(silu_ready, 1)
                if kind == "fill" and a[0]["eng"] == "dve":
                    f = a[0]
                    what, args = f["kind"], f["args"]
                    ps = take(f)
                    if what == "ada":
                        m = args[0]
                        sh, sc = ((SH_MSA, SC_MSA), (SH_MLP, SC_MLP))[m]
                        w, bb = ("ln1_w", "ln1_b") if m == 0 else ("ln2_w", "ln2_b")
                        for k in range(KT):
                            p_sh, p_sc = ps[:, B * k:B * k + B], ps[:, B * (KT + k):B * (KT + k) + B]
                            one = adab1[:, sc * KT + k:sc * KT + k + 1]
                            dve.tensor_scalar(LA[:, m, k, :], p_sc, one, col(w, k), ALU.add, ALU.mult)
                            link(dve.tensor_scalar(lt[:, k, :], p_sc, one, col(bb, k), ALU.add, ALU.mult))
                            link(dve.scalar_tensor_tensor(out=LB[:, m, k, :], in0=p_sh, scalar=col("ada_b", sh * KT + k),
                                                          in1=lt[:, k, :], op0=ALU.add, op1=ALU.add))
                        dve.tensor_copy(lt[:, :, :], LA[:, m, :, :]).then_inc(affine, 1)
                        dve.wait_ge(affine, m + 1)
                        dve.tensor_copy(lt[:, :, :], LA[:, m, :, :]).then_inc(rel["dve"], 1)
                        if m == 0:
                            dve.wait_ge(consts, 2)
                            for k in range(KT):
                                for b in range(B):
                                    mm = dve.tensor_scalar(silu_wide[:, k, b, :], ident[:, :], 0.0,
                                                           silu[:, k * B + b:k * B + b + 1], ALU.mult, ALU.add)
                            mm.then_inc(silu_ready, 1)
                            dve.wait_ge(wq_hi, 1)
                            dve.wait_ge(wq_in, 16)
                            dve.tensor_tensor(wqkv_l[:, :, :], w_qraw, wqkv_h[:, :, :].bitcast(F32),
                                              ALU.subtract).then_inc(wq_split, 1)
                    elif what == "gate":
                        b, m = args
                        dve.wait_ge(trows_in, 16)
                        dve.tensor_tensor(GATE[:, b, m, :], ps[:, 0:C], TR[:, TROW_AMLP if m else TROW_AMSA, :],
                                          ALU.add).then_inc(rel["dve"], 1)
                    elif what == "v":
                        b, t = args
                        k = b * TT + t
                        dve.wait_ge(rows_in, 16)
                        if b >= 1:
                            dve.wait_ge(v_ready, TT * b)
                        dve.tensor_tensor(VT[:, t, :], ps[:, 0:C], RW[:, ROW_BV, :], ALU.add).then_inc(rel["dve"], 1)
                    elif what == "max":
                        b, g, j, t = args
                        n = b * G + g
                        if (j, t) == (0, 0) and n >= 1:
                            dve.wait_ge(maxed, n)
                        pos = 2 * (j % 2) + j // 2
                        dve.tensor_reduce(nm[:, t, pos:pos + 1], ps[:, :], AX.X, ALU.max,
                                          negate=True).then_inc(rel["dve"], 1)
                        if (j, t) == (GH - 1, TT - 1):
                            dve.wait_ge(rel["dve"], f["count"])
                            if n >= 1:
                                dve.wait_ge(filled, find("maxrow", *divmod(n - 1, G))["n"] + 1)
                            nmv = nm[:, :, :].rearrange("p t (a l) -> p t a l", a=2)
                            msv = ms[:, :, :].rearrange("p t (a s l) -> p t a s l", a=2, s=2)
                            for half in range(2):
                                ins = dve.tensor_copy(msv[:, :, half, 0, :], nmv[:, :, half, :])
                            link(ins)
                            for half in range(2):
                                ins = dve.tensor_tensor(msv[:, :, half, 1, :], nmv[:, :, half, :],
                                                        msv[:, :, half, 0, :].bitcast(F32), ALU.subtract)
                            ins.then_inc(maxed, 1)
                    elif what == "proj":
                        b, t = args
                        dve.wait_ge(gate_ready, 2 * B)
                        dve.wait_ge(res1, b + 1)
                        xt = X[:, b * TT + t, :]
                        if t >= 1:
                            dve.wait_ge(x2_ready, b * TT + t)
                        elif b >= 1:
                            dve.wait_ge(y_ready, b * TT)
                        dve.tensor_tensor(PT[:, :], ps[:, 0:C], GATE[:, b, 0, :], ALU.mult).then_inc(rel["dve"], 1)
                        dve.wait_ge(rel["dve"], f["count"])
                        dve.tensor_tensor(xt, PT[:, :], xt, ALU.add).then_inc(x2_ready, 1)
                    elif what == "fc2":
                        b, t = args
                        k = b * TT + t
                        dve.wait_ge(res2, b + 1)
                        if t == 0:
                            dve.wait_ge(x2_ready, (b + 1) * TT)
                        else:
                            dve.wait_ge(y_ready, k)
                        dve.tensor_tensor(PT[:, :], ps[:, 0:C], GATE[:, b, 1, :], ALU.mult).then_inc(rel["dve"], 1)
                        dve.wait_ge(rel["dve"], f["count"])
                        dve.tensor_tensor(X[:, k, :], PT[:, :], X[:, k, :], ALU.add).then_inc(y_ready, 1)
                if kind == "gelu_b":
                    f = a[0]
                    q = f["gelu"]
                    dve.wait_ge(rel["act"], f["count"])
                    dve.scalar_tensor_tensor(out=VG[:, q % 2, :, :], in0=VG[:, q % 2, :, :], scalar=1.0 / GELU_CUBIC,
                                             in1=XG[:, q % 2, :, :], op0=ALU.add, op1=ALU.mult).then_inc(g_mid, 1)
                if kind == "gelu_d":
                    q = a[0]["gelu"]
                    dve.wait_ge(g_tanh, q + 1)
                    dve.scalar_tensor_tensor(out=VG[:, q % 2, :, :], in0=VG[:, q % 2, :, :], scalar=1.0,
                                             in1=XG[:, q % 2, :, :], op0=ALU.add, op1=ALU.mult).then_inc(g_full, 1)
                if kind in ("ln1", "ln2"):
                    b = a[0]
                    seen = ln_order.index((kind, b))
                    if kind == "ln1":
                        dve.wait_ge(x_in[b], 16)
                    else:
                        dve.wait_ge(x2_ready, TT * (b + 1))
                    for t in range(TT):
                        ins = dve.bn_stats(st6[:, t, :], X[:, b * TT + t, :])
                    link(ins)
                    for t in range(TT):
                        ins = dve.bn_aggr(mv[:, t, :], st6[:, t, :])
                    link(ins)
                    if seen >= 1:
                        dve.wait_ge(normed, seen)
                    link(dve.tensor_scalar(ve[:, :], mv[:, :, 1], EPS, None, ALU.add))
                    link(dve.tensor_scalar(rs[:, :].bitcast(I32), ve[:, :].bitcast(I32), -0.5, RSQRT_SEED,
                                           ALU.mult, ALU.add))
                    for _ in range(3):
                        link(dve.tensor_tensor(rt[:, :], rs[:, :], rs[:, :], ALU.mult))
                        link(dve.scalar_tensor_tensor(out=rt[:, :], in0=rt[:, :], scalar=-0.5, in1=ve[:, :],
                                                      op0=ALU.mult, op1=ALU.mult))
                        link(dve.scalar_tensor_tensor(out=rs[:, :], in0=rt[:, :], scalar=1.5, in1=rs[:, :],
                                                      op0=ALU.add, op1=ALU.mult))
                    dve.scalar_tensor_tensor(out=nmr[:, :], in0=mv[:, :, 0], scalar=-1.0, in1=rs[:, :],
                                             op0=ALU.mult, op1=ALU.mult).then_inc(stats, 1)
                if kind == "normalise":
                    b = a[0]
                    dve.wait_ge(o_in, 32 * G * (b + 1))
                    dve.reciprocal(LC[:, :, :], LC[:, :, :]).then_inc(recip, 1)

        @block.gpsimd
        def _(pool):
            seq = [0]

            def link(ins):
                seq[0] += 1
                ins.then_inc(pool_seq, 1)
                pool.wait_ge(pool_seq, seq[0])

            def lo(dst, full, hi):
                return pool.tensor_tensor(dst, full, hi.bitcast(F32), ALU.subtract)

            def lo_of_weights(raw, h, l):
                link(pool.tensor_copy(h, raw))
                lo(l, raw, h).then_inc(w_split, 1)

            for kind, a in plan:
                if kind == "setup":
                    pool.memset(ident[:, :], 0.0).then_inc(consts, 1)
                    pool.wait_ge(consts, 1)
                    pool.affine_select(out=ident[:, :], in_=ident[:, :], compare_op=ALU.not_equal, fill=1.0,
                                       base=0, pattern=[[-1, P]], channel_multiplier=1).then_inc(consts, 1)
                    pool.memset(MR[:, :].bitcast(F32), 1.0).then_inc(consts, 1)
                    pool.memset(VA[:, :, :, :], 1.0).then_inc(pool_seq, 1)
                    seq[0] += 1
                    pool.wait_ge(pool_seq, seq[0])
                if kind in ("ln1", "ln2"):
                    b = a[0]
                    seen = ln_order.index((kind, b))
                    pool.wait_ge(stats, seen + 1)
                    if seen >= 1:
                        k0, b0 = ln_order[seen - 1]
                        pool.wait_ge(filled, find("turn" + k0[-1], b0, KT - 1)["n"] + 1)
                    for t in range(TT):
                        ins = pool.tensor_scalar(NRM[:, t, :], X[:, b * TT + t, :], rs[:, t:t + 1], nmr[:, t:t + 1],
                                                 ALU.mult, ALU.add)
                    ins.then_inc(normed, 1)
                if kind == "residual1" or kind == "residual2":
                    b, m = a[0], int(kind[-1]) - 1
                    pool.wait_ge(normed, ln_order.index(("ln" + kind[-1], b)) + 1)
                    pool.wait_ge(gate_ready, 2 * B)
                    at = res_order.index((kind, b))
                    if at >= 1:
                        k0, b0 = res_order[at - 1]
                        pool.wait_ge(res2 if k0 == "residual2" else res1, b0 + 1)
                    link(pool.tensor_tensor(GB[:, :], GATE[:, b, m, :], RW[:, ROW_B2 if m else ROW_BP, :], ALU.mult))
                    for t in range(TT):
                        ins = pool.tensor_tensor(X[:, b * TT + t, :], X[:, b * TT + t, :], GB[:, :], ALU.add)
                    ins.then_inc(res2 if m else res1, 1)
                if kind == "weights":
                    i = a[0]
                    if i == 0:
                        pool.wait_ge(wp_in, 16)
                        lo_of_weights(w_praw[:, :, :], wp_h[:, :, :], wp_l[:, :, :])
                    if i in (1, 2):
                        pool.wait_ge(w1_in, 16)
                        lo_of_weights(w_1raw[:, i - 1, :], w1_h[:, i - 1, :], w1_l[:, i - 1, :])
                    if i in (3, 4):
                        pool.wait_ge(w2_in, 16)
                        k = slice((i - 3) * FN // 2, (i - 2) * FN // 2)
                        lo_of_weights(w_2raw[:, k, :], w2_h[:, k, :], w2_l[:, k, :])
                if kind == "fill":
                    f = a[0]
                    what, args = f["kind"], f["args"]
                    if what in ("turn1", "turn2", "qk"):
                        pool.wait_ge(rel["act"], f["count"])
                        if what == "qk":
                            h, l = (QK[:, args[1], i, :] for i in range(2))
                        else:
                            t = HT if what == "turn1" else AH
                            h, l = (t[:, i, args[1], :] for i in range(2))
                        lo(l, FULL[:, f["split"] % 2, :], h).then_inc(split, 1)
                    if what == "gate":
                        b, m = args
                        if (b, m) == (0, 0):
                            pool.wait_ge(trows_in, 16)
                            pool.wait_ge(rows_in, 16)
                            link(pool.tensor_tensor(TR[:, TROW_G1, :], TR[:, TROW_G1, :], TR[:, TROW_GO, :], ALU.mult))
                            link(pool.tensor_scalar(TR[:, TROW_G2, :], TR[:, TROW_G2, :], 0.5, 1.0, ALU.mult, ALU.mult))
                            link(pool.tensor_scalar(RW[:, ROW_B2, :], RW[:, ROW_B2, :], 2.0, 1.0, ALU.mult, ALU.mult))
                        pool.wait_ge(rel["dve"], f["count"])
                        pool.tensor_tensor(GATE[:, b, m, :], GATE[:, b, m, :], TR[:, TROW_G2 if m else TROW_G1, :],
                                           ALU.mult).then_inc(gate_ready, 1)
                if kind == "v_place":
                    b = a[0]
                    pool.wait_ge(rows_in, 16)
                    if b >= 1:
                        pool.wait_ge(valued, G * TT * b)
                    for t in range(TT):
                        pool.wait_ge(rel["dve"], find("v", b, t)["count"])
                        pool.tensor_tensor(VA[:, t, :, 0:2 * D:2],
                                           VT[:, t, :].rearrange("p (h d) -> p h d", h=H),
                                           RW[:, ROW_GV, :].rearrange("p (h d) -> p h d", h=H),
                                           ALU.mult).then_inc(v_ready, 1)
                if kind == "gelu_d":
                    f = a[0]
                    b, half, i = f["args"]
                    q = f["gelu"]
                    pool.wait_ge(g_full, q + 1)
                    if i == 0 and (b, half) != (0, 0):
                        b0, h0 = (b, 0) if half else (b - 1, 1)
                        pool.wait_ge(filled, find("fc2", b0, 2 * h0 + 1)["n"] + 1)
                    if q == 0:
                        pool.wait_ge(w_split, 5)
                    u = [U[:, k, 2 * i:2 * i + 2, :] for k in range(2)]
                    link(pool.tensor_copy(u[0], VG[:, q % 2, :, :]))
                    lo(u[1], VG[:, q % 2, :, :], u[0]).then_inc(u_ready, 1)
                if kind == "normalise":
                    b = a[0]
                    pool.wait_ge(recip, b + 1)
                    pool.tensor_tensor(OC[:, :, :], OC[:, :, :], LC[:, :, :], ALU.mult).then_inc(attn_full, 1)
                    pool.wait_ge(attn_hi, b + 1)
                    lo(AH[:, 1, :, :], OC[:, :, :], AH[:, 0, :, :]).then_inc(attn_split, 1)


def kernel(x, cond_1024, L0_cond_ln1_w, L0_cond_ln1_b, L0_cond_ln2_w, L0_cond_ln2_b, L0_cond_gamma_qkv,
           L0_cond_gamma_attn_out, L0_cond_w_qkv, L0_cond_b_qkv, L0_cond_w_proj, L0_cond_b_proj, L0_cond_w_fc1,
           L0_cond_b_fc1, L0_cond_w_fc2, L0_cond_b_fc2, L0_cond_w_ada, L0_cond_b_ada, L0_cond_gamma1,
           L0_cond_gamma2):
    import numpy as np
    import concourse.bacc as bacc
    from concourse.bass_utils import run_bass_kernel_spmd as run

    def spread(w):
        w = np.asarray(w)
        lead = w.shape[:-1]
        w = w.reshape(*lead, KT, 4, 2, D)
        return np.moveaxis(w, -3, -1).reshape(*lead, C)

    def tiles(v):
        return np.asarray(v).reshape(-1, P).T

    w_qkv, b_qkv, g_qkv = (np.asarray(v) for v in (L0_cond_w_qkv, L0_cond_b_qkv, L0_cond_gamma_qkv))
    w = np.concatenate([spread(w_qkv[:, 0:C]), spread(w_qkv[:, C:2 * C]), w_qkv[:, 2 * C:]], axis=1)
    qk = [np.concatenate([spread(v[0:C]), spread(v[C:2 * C])]) for v in (b_qkv, g_qkv)]
    cond = np.asarray(cond_1024).reshape(B, KT, P).transpose(2, 1, 0).reshape(P, KT * B)
    cols = np.concatenate([tiles(qk[0]), tiles(qk[1]), tiles(L0_cond_ln1_w), tiles(L0_cond_ln1_b),
                           tiles(L0_cond_ln2_w), tiles(L0_cond_ln2_b), tiles(L0_cond_b_fc1),
                           tiles(L0_cond_b_ada), cond], axis=1)
    b_ada = np.asarray(L0_cond_b_ada).reshape(6, C)
    rows = np.concatenate([b_qkv[2 * C:], g_qkv[2 * C:], np.asarray(L0_cond_b_proj), np.asarray(L0_cond_b_fc2)])
    trows = np.concatenate([np.asarray(L0_cond_gamma1), np.asarray(L0_cond_gamma_attn_out),
                            np.asarray(L0_cond_gamma2), b_ada[G_MSA], b_ada[G_MLP]])
    w_ada = np.asarray(L0_cond_w_ada)
    arrays = {"x": np.asarray(x), "cols": cols, "rows": rows[None, :], "trows": trows[None, :], "w_qkv": w,
              "w_proj": np.asarray(L0_cond_w_proj), "w_fc1": np.asarray(L0_cond_w_fc1),
              "w_fc2": np.asarray(L0_cond_w_fc2), "w_ada": w_ada}
    nc = bacc.Bacc("TRN2", target_bir_lowering=False, num_devices=1)
    arrays = {k: np.ascontiguousarray(v) for k, v in arrays.items()}
    ins = {k: nc.dram_tensor("in_" + k, v.shape, F32, kind="ExternalInput").ap() for k, v in arrays.items()}
    y = nc.dram_tensor("y", (B, N, C), F32, kind="ExternalOutput").ap()
    block_program(nc, out=y, **ins)
    r = run(nc, [{"in_" + k: v for k, v in arrays.items()}], core_ids=[0])
    return r.results[0]["y"]
```

```python
from contextlib import ExitStack

import concourse.bass as bass
from concourse import mybir

F32 = mybir.dt.float32
F32R = mybir.dt.float32r
I32 = mybir.dt.int32
ALU = mybir.AluOpType
ACT = mybir.ActivationFunctionType
AX = mybir.AxisListType

P = 128
B, N, C, H = 4, 512, 256, 16
D = C // H
MLP = 4 * C
KT = C // P
TT = N // P
NT = B * TT
G = 4
GH = H // G
FN = MLP // P
HALF = N // 2
STEPS = B * G * TT
RING = 3
EPS = 1e-6
GELU_CUBIC = 0.044715
GELU_SCALE = 0.7978845608028654
RSQRT_SEED = 1597463007.0
QROWS, MROWS = 3 * D, 2

COLS = {}
for _name, _n in (("qk_b", 4), ("qk_g", 4), ("ln1_w", 2), ("ln1_b", 2), ("ln2_w", 2), ("ln2_b", 2),
                  ("fc1_b", FN), ("ada_b", 12), ("cond", 2 * B)):
    COLS[_name] = (sum(n for _, n in COLS.values()), _n)
NCOLS = sum(n for _, n in COLS.values())
ROW_BV, ROW_GV, ROW_BP, ROW_B2 = range(4)
TROW_G1, TROW_GO, TROW_G2, TROW_AMSA, TROW_AMLP = range(5)
SH_MSA, SC_MSA, G_MSA, SH_MLP, SC_MLP, G_MLP = range(6)


MATMULS = {"qk": 3 * KT, "v": 3 * KT, "proj": 3 * KT, "fc1": 6 * KT, "fc2": 3 * FN}

AHEAD = {
    "turn1": (0.01, 0.49),
    "v": (1.04, 1.54, 2.72, 2.76),
    "qk0": (3.75, 4.85),
    "qk1": (15.81, 15.9),
    "residual1": (3.59,),
    "qk_rows0": (7.6,),
    "qk_rows1": (16.74,),
}
STATS1, LN1 = (7.15, 9.55, 11.03, 11.73), 11.8
BEHIND = {
    "proj": (2.88, 3.37, 3.42, 3.7),
    "stats": (3.51, 3.7, 3.93, 3.96),
    "ln2": (4.33,),
    "turn2": (5.36, 5.63),
    "residual2": (5.89,),
    "fc1": (6.31, 7.03, 7.56, 8.35, 9.6, 11.18, 11.57, 12.53),
    "fc2": (9.86, 10.13, 14.19, 15.42),
}
GELU = (0.31, 0.39, 0.86)
FC2_PARTS, FC2_EVERY = 3, 0.06
RECIP = ((11.83, 12.66), (17.29, 17.44))
DIVIDE = ((12.18, 14.48), (17.44, 18.26))
ATTN_HI = ((13.99, 14.26), (17.8, 18.44))
ATTN_LO = ((12.72, 14.19), (15.44, 15.67))
GATES = (0.81, 1.78, 1.92, 2.7, 3.25, 3.54, 4.31, 5.31)
ADA1, RESIDUAL_0, LOAD_MLP = 5.78, 8.77, 7.94
WEIGHTS = (7.85, 12.13, 12.28, 13.74, 14.82)
TAIL = {
    "proj": (2.67, 3.15, 3.22, 3.34),
    "ln2": (3.55,),
    "turn2": (3.73, 3.74),
    "residual2": (4.38,),
    "fc1": (3.92, 4.36, 5.16, 5.86, 6.67, 7.52, 7.87, 8.2),
    "fc2": (9.76, 10.87, 14.29, 15.46),
}
TAIL_GELU = (0.39, 0.92, 1.31)
SCORES1, VALUES = 0.33, 0.67
MAXES, MAXROW = 2.85, 3.33


TAIL_DVE_LO = tuple((B - 1) * FN + i for i in range(0, FN, 2))


def make_plan():
    plan, fills = [], []
    counts = {}

    def count(*key):
        counts[key] = counts.get(key, 0) + 1
        return counts[key]

    def do(kind, *args):
        plan.append((kind, args))

    def fill(kind, *args, lo="pool", part=0, parts=1):
        if parts > 1:
            m = MATMULS[kind]
            do("part", kind, args, len(fills), m * part // parts, m * (part + 1) // parts)
            if part < parts - 1:
                return None
        eng = "act" if kind in ("turn1", "turn2", "qk", "maxrow", "fc1") else "dve"
        f = {"kind": kind, "args": args, "n": len(fills), "slot": len(fills) % RING,
             "eng": eng, "count": count("took", eng), "parted": parts > 1}
        if kind in ("turn1", "turn2", "qk"):
            f["split"] = count("split") - 1
            f["lo"], f["lo_count"] = lo, count("lo", lo)
        if kind == "fc1":
            f["gelu"] = count("gelu") - 1
            f["ulo"] = "dve" if f["gelu"] in TAIL_DVE_LO else "pool"
            f["ulo_count"] = count("ulo", f["ulo"])
            f["buffer"] = f["gelu"] % 2 if args[0] < B - 1 else 2 + f["gelu"] % 4
        fills.append(f)
        plan.append(("fill", (f,)))
        return f

    def maxes(n):
        b, g = divmod(n, G)
        return [("max", b, g, j, t) for t in range(TT) for j in range(GH)]

    def stats(m, b):
        for t in range(TT):
            do("stats", m, b, t)

    def norm_tokens(m, b, eng="pool"):
        do("ln", {"m": m, "b": b, "n": count("ln") - 1, "eng": eng, "count": count("ln", eng)})

    def division(b, T, c, eng="pool"):
        return {"b": b, "T": T, "c": c, "eng": eng, "count": count("division", eng),
                "n": count("division") - 1}

    do("setup")
    stats(0, 0)
    norm_tokens(0, 0, "dve")
    fill("ada", 0)
    fill("turn1", 0, 0)
    fill("turn1", 0, 1, lo="dve")
    do("silu_wide")
    do("wq_lo")
    do("lo", fills[-1])
    fill("qk", 0, 0, 0)
    fill("qk", 0, 1, 0, lo="dve")
    do("lo", fills[-1])
    do("qk_rows", 0, 0)
    for t in range(TT):
        fill("v", 0, t)
    do("v_place", 0)
    fill("qk", 0, 0, 1)
    fill("qk", 0, 1, 1)
    do("qk_rows", 0, 1)
    stats(0, 1)
    norm_tokens(0, 1)
    gates = [("gate", b, m) for b in range(B) for m in range(2)]
    for m in maxes(0):
        fill(*m)
    fill("maxrow", 0, 0)

    timed = []

    def at(position, kind, *args):
        timed.append((position, len(timed), kind, args))

    for s in range(STEPS):
        b, i = divmod(s, G * TT)
        n, kt = divmod(s, TT)
        at(s, "scores", s, 0)
        at(s + SCORES1, "scores", s, 1)
        if s >= 1:
            at(s + VALUES, "values", s - 1)
        if i == 0 and b >= 1:
            at(s + VALUES, "v_place", b)
        if kt == 0 and s >= 1:
            at(s + VALUES, "attn_out", n - 1)
        if kt == 0 and n + 1 < B * G:
            for k, m in enumerate(maxes(n + 1)):
                at(s + (k + 0.5) * MAXES / (GH * TT), *m)
            at(s + MAXROW, "maxrow", *divmod(n + 1, G))
    for b in range(B):
        t0 = b * G * TT
        nb, pb = b + 1, b - 1
        if nb < B:
            for k in range(KT):
                at(t0 + AHEAD["turn1"][k], "turn1", nb, k)
            for t in range(TT):
                at(t0 + AHEAD["v"][t], "v", nb, t)
            for mt in range(2):
                for which in range(2):
                    at(t0 + AHEAD[f"qk{mt}"][which], "qk", nb, which, mt)
                at(t0 + AHEAD[f"qk_rows{mt}"][0], "qk_rows", nb, mt)
            at(t0 + AHEAD["residual1"][0], "residual1", nb)
        if nb + 1 < B:
            for t in range(TT):
                at(t0 + STATS1[t], "stats", 0, nb + 1, t)
            at(t0 + LN1, "norm_tokens", 0, nb + 1)
        if b == 0:
            for k, g in enumerate(gates):
                at(GATES[k], *g)
            at(ADA1, "ada", 1)
            at(RESIDUAL_0, "residual1", 0)
            at(LOAD_MLP, "load_mlp")
            for k in range(5):
                at(WEIGHTS[k], "weights", k)
        for T in range(2):
            for c in range(2):
                if (b, T) < (B - 1, 1):
                    at(t0 + RECIP[T][c], "recip", b, T, c)
                    at(t0 + DIVIDE[T][c], "divide", b, T, c)
        if pb >= 0:
            for t in range(TT):
                at(t0 + BEHIND["proj"][t], "proj", pb, t)
                at(t0 + BEHIND["stats"][t], "stats", 1, pb, t)
                at(t0 + BEHIND["fc2"][t], "fc2", pb, t)
            at(t0 + BEHIND["ln2"][0], "norm_tokens", 1, pb)
            for k in range(KT):
                at(t0 + BEHIND["turn2"][k], "turn2", pb, k)
            at(t0 + BEHIND["residual2"][0], "residual2", pb)
            for k in range(FN):
                at(t0 + BEHIND["fc1"][k], "fc1", pb, k // 4, k % 4)

    last = B - 1
    for position, kind, *args in (
            (0.0, "values", STEPS - 1), (0.1, "attn_out", B * G - 1),
            (1.0, "recip", last, 1, 0), (1.1, "divide", last, 1, 0), (1.3, "recip", last, 1, 1),
            (1.7, "divide", last, 1, 1), (TAIL["ln2"][0], "norm_tokens", 1, last, "dve"),
            (TAIL["residual2"][0], "residual2", last)):
        at(STEPS + position, kind, *args)
    for t in range(TT):
        at(STEPS + TAIL["proj"][t], "proj", last, t)
        at(STEPS + TAIL["proj"][t] + 0.01, "stats", 1, last, t)
        at(STEPS + TAIL["fc2"][t], "fc2", last, t)
    for k in range(KT):
        at(STEPS + TAIL["turn2"][k], "turn2", last, k)
    for k in range(FN):
        at(STEPS + TAIL["fc1"][k], "fc1", last, k // 4, k % 4)

    opened, held = None, []
    while timed or held:
        if held and not opened:
            position, _, kind, args = held.pop(0)
        else:
            timed.sort()
            position, _, kind, args = timed.pop(0)
        is_fill = kind in ("turn1", "turn2", "qk", "v", "proj", "fc1", "fc2", "max", "maxrow", "gate", "ada")
        if opened and is_fill:
            held.append((position, 0, kind, args))
        elif kind == "norm_tokens":
            norm_tokens(*args)
        elif kind == "divide":
            b, T, c = args
            tail = (b, T) == (last, 1)
            x = division(*args, eng="dve" if tail else "pool")
            do("divide", x)
            at(position + 0.3 if tail else b * G * TT + ATTN_HI[T][c], "attn_hi", x)
            at(position + 0.5 if tail else b * G * TT + ATTN_LO[T][c], "attn_lo", x)
        elif kind == "fc2" and FC2_PARTS > 1 and args[0] < last:
            opened = args
            fill(kind, *args, part=0, parts=FC2_PARTS)
            for k in range(1, FC2_PARTS):
                at(position + k * FC2_EVERY, "more", kind, args, k)
        elif kind == "more":
            kind, args, k = args
            fill(kind, *args, part=k, parts=FC2_PARTS)
            if k == FC2_PARTS - 1:
                opened = None
        elif is_fill:
            tail_lo = "dve" if (kind, args) == ("turn2", (last, 1)) else "pool"
            f = fill(kind, *args, lo=tail_lo)
            if tail_lo == "dve":
                at(position + 0.1, "lo", f)
            if kind == "fc1":
                for k, name in enumerate(("gelu_b", "gelu_c", "gelu_d")):
                    at(position + (TAIL_GELU if args[0] == last else GELU)[k], name, f)
                at(position + (TAIL_GELU if args[0] == last else GELU)[2] + 0.02, "gelu_lo", f)
        else:
            do(kind, *args)
    return plan, fills


def block_program(nc, x, cols, rows, trows, w_qkv, w_proj, w_fc1, w_fc2, w_ada, out):
    plan, fills = make_plan()

    def find(kind, *args):
        for f in fills:
            if f["kind"] == kind and f["args"] == args:
                return f
        raise KeyError((kind, args))

    with ExitStack() as ctx:
        def sb(name, shape, dt=F32):
            return ctx.enter_context(nc.sbuf_tensor(name, shape, dt))

        def sem(name):
            return ctx.enter_context(nc.semaphore(name))

        X = sb("X", [P, NT, C])
        wqkv_h, wqkv_l = sb("wqkv_h", [P, KT, 3 * C], F32R), sb("wqkv_l", [P, KT, 3 * C], F32R)
        wp_h, wp_l = sb("wp_h", [P, KT, C], F32R), sb("wp_l", [P, KT, C], F32R)
        w1_h, w1_l = sb("w1_h", [P, KT, MLP], F32R), sb("w1_l", [P, KT, MLP], F32R)
        w2_h, w2_l = sb("w2_h", [P, FN, C], F32R), sb("w2_l", [P, FN, C], F32R)
        QA = sb("QA", [P, H // 2, N], F32R)
        KA = sb("KA", [P, H // 2, N], F32R)
        QK = sb("QK", [P, 2, 2, N], F32R)
        PB = sb("PB", [P, 2, GH, N])
        VA = sb("VA", [P, TT, H, 2 * D])
        HT = sb("HT", [P, 2, KT, N], F32R)
        AH = sb("AH", [P, 2, KT, N], F32R)
        FULL = sb("FULL", [P, 2, N])
        NRM = sb("NRM", [P, TT, C])
        OS = sb("OS", [P, N])
        OC = sb("OC", [P, KT, N])
        LC = sb("LC", [P, KT, N])
        RW = sb("RW", [P, 4, C])
        GATE = sb("GATE", [P, B, 2, C])
        GB = sb("GB", [P, C])
        XV = sb("XV", [P, 2, 2, 2, HALF])
        PB_halves = PB[:, :, :, :].rearrange("p s j n -> p (s j n)").rearrange("p (q a e n) -> p a q e n", q=4, a=2, e=2)
        XV_flat = XV[:, :, :, :, :].rearrange("p a q e n -> p (a q e n)")
        TR = XV_flat[:, 0:5 * C].rearrange("p (r c) -> p r c", r=5)
        w_praw = XV_flat[:, 5 * C:7 * C].rearrange("p (k c) -> p k c", k=KT)
        VT = sb("VT", [P, TT, C])
        PT = sb("PT", [P, C])
        ident = sb("ident", [P, P])
        MR = sb("MR", [2 * GH, N], F32R)
        nm = sb("nm", [P, TT, GH])
        ms = sb("ms", [P, TT, 2 * GH], F32R)
        PC = sb("PC", [P, NCOLS])
        qkb = sb("qkb", [P, 4])
        qkg = sb("qkg", [P, 4])
        adab1 = sb("adab1", [P, 12])
        silu = sb("silu", [P, 2 * B])
        tnh = sb("tnh", [P, 2 * B])
        LA = sb("LA", [P, 2, KT, B])
        LB = sb("LB", [P, 2, KT, B])
        lt = sb("lt", [P, KT, B])
        st6 = sb("st6", [P, TT, 6])
        mv = sb("mv", [P, TT, 2])
        ve = sb("ve", [P, TT])
        rs = sb("rs", [P, TT])
        rt = sb("rt", [P, TT])
        nmr = sb("nmr", [P, TT])
        with nc.sbuf_tensor("w_adaraw", [P, KT, 6 * C], F32) as w_adaraw, \
                nc.sbuf_tensor("silu_wide", [P, KT, B, P], F32) as silu_wide:
            pass
        with nc.sbuf_tensor("w_1raw", [P, KT, MLP], F32) as w_1raw, \
                nc.sbuf_tensor("w_2raw", [P, FN, C], F32) as w_2raw:
            pass
        U = sb("U", [P, 2, FN, HALF], F32R)
        U_last = QA[:, :, :].rearrange("p j n -> p (j n)").rearrange("p (l k n) -> p l k n", l=2, k=FN)
        w_qraw = PB[:, 1, :, :].rearrange("p j n -> p (j n)")[:, 0:KT * 3 * C].rearrange("p (k n) -> p k n", k=KT)

        ST = [ctx.enter_context(nc.psum_tensor(f"ST{i}", [P, 2, N], F32)) for i in range(2)]
        SM = [ctx.enter_context(nc.psum_tensor(f"SM{i}", [P, N], F32)) for i in range(RING)]
        O = ctx.enter_context(nc.psum_tensor("O", [P, N], F32))

        cols_in, rows_in, trows_in, ada0_in, ada1_in = map(sem, ("cols_in", "rows_in", "trows_in", "ada0_in", "ada1_in"))
        wq_in, wp_in, w1_in, w2_in, ones_in = map(sem, ("wq_in", "wp_in", "w1_in", "w2_in", "ones_in"))
        x_in = [sem(f"x_in{b}") for b in range(B)]
        consts = sem("consts")
        pool_seq = sem("pool_seq")
        tanh_c = sem("tanh_c")
        dve_seq = sem("dve_seq")
        silu_ready = sem("silu_ready")
        wq_hi, wq_split = sem("wq_hi"), sem("wq_split")
        w_hi, w_split = sem("w_hi"), sem("w_split")
        filled = sem("filled")
        rel = {"act": sem("act_took"), "dve": sem("dve_took")}
        stats_done, aggregated = sem("stats_done"), sem("aggregated")
        affine = sem("affine")
        seeded = sem("seeded")
        normed = {"pool": sem("pool_normed"), "dve": sem("dve_normed")}
        split = {"pool": sem("pool_split"), "dve": sem("dve_split")}
        qk_in = [sem("qk_in0"), sem("qk_in1")]
        mrow_in = [sem("mrow_in0"), sem("mrow_in1")]
        maxed = sem("maxed")
        v_biased, v_ready = sem("v_biased"), sem("v_ready")
        scored, exped, valued = sem("scored"), sem("exped"), sem("valued")
        o_copied, o_in = sem("o_copied"), sem("o_in")
        recip, attn_hi = sem("recip"), sem("attn_hi")
        attn_full = {"pool": sem("pool_attn_full"), "dve": sem("dve_attn_full")}
        attn_split = {"pool": sem("pool_attn_split"), "dve": sem("dve_attn_split")}
        gate_raw, gate_ready = sem("gate_raw"), sem("gate_ready")
        biased = sem("biased")
        x2_ready = sem("x2_ready")
        g_mid, g_tanh, g_full = map(sem, ("g_mid", "g_tanh", "g_full"))
        u_ready = {"pool": sem("pool_u_ready"), "dve": sem("dve_u_ready")}
        y_ready, y_out = sem("y_ready"), sem("y_out")

        def col(name, i, n=1):
            return PC[:, COLS[name][0] + i:COLS[name][0] + i + n]

        def half_rows(h):
            return 64 * (h % 2)

        def weight_parts(i):
            if i == 0:
                return w_praw[:, :, :], wp_h[:, :, :], wp_l[:, :, :]
            if i in (1, 2):
                return w_1raw[:, i - 1, :], w1_h[:, i - 1, :], w1_l[:, i - 1, :]
            k = slice((i - 3) * FN // 2, (i - 2) * FN // 2)
            return w_2raw[:, k, :], w2_h[:, k, :], w2_l[:, k, :]

        def gelu_buffers(f):
            q = f["buffer"]
            return [XV[:, a, q, :, :] if q < 2 else PB_halves[:, a, q - 2, :, :] for a in range(2)]

        def gelu_output(b, half):
            return U_last if (b, half) == (B - 1, 1) else U

        def wait_gelu(e, f):
            e.wait_ge(u_ready[f["ulo"]], f["ulo_count"])

        def write_gelu_lo(e, f):
            b, half, i = f["args"]
            u = [gelu_output(b, half)[:, k, 2 * i:2 * i + 2, :] for k in range(2)]
            e.wait_ge(g_full, f["gelu"] + 1)
            e.tensor_tensor(u[1], gelu_buffers(f)[1], u[0].bitcast(F32), ALU.subtract).then_inc(u_ready[f["ulo"]], 1)

        def split_tile(f):
            if f["kind"] == "qk":
                return [QK[:, f["args"][1], i, :] for i in range(2)]
            t = HT if f["kind"] == "turn1" else AH
            return [t[:, i, f["args"][1], :] for i in range(2)]

        def divide(e, x):
            T, cs = x["T"], slice(x["c"] * HALF, (x["c"] + 1) * HALF)
            e.wait_ge(recip, x["n"] + 1)
            e.tensor_tensor(OC[:, T, cs], OC[:, T, cs], LC[:, T, cs], ALU.mult).then_inc(attn_full[x["eng"]], 1)

        def divide_lo(e, x):
            T, cs = x["T"], slice(x["c"] * HALF, (x["c"] + 1) * HALF)
            e.wait_ge(attn_hi, x["n"] + 1)
            e.wait_ge(attn_full[x["eng"]], x["count"])
            e.tensor_tensor(AH[:, 1, T, cs], OC[:, T, cs], AH[:, 0, T, cs].bitcast(F32),
                            ALU.subtract).then_inc(attn_split[x["eng"]], 1)

        def newton(e, link):
            for _ in range(3):
                link(e.tensor_tensor(rt[:, :], rs[:, :], rs[:, :], ALU.mult))
                link(e.tensor_tensor(rt[:, :], rt[:, :], ve[:, :], ALU.mult))
                link(e.tensor_scalar(rt[:, :], rt[:, :], -0.5, 1.5, ALU.mult, ALU.add))
                link(e.tensor_tensor(rs[:, :], rs[:, :], rt[:, :], ALU.mult))
            link(e.tensor_tensor(nmr[:, :], mv[:, :, 0], rs[:, :], ALU.mult))
            link(e.tensor_scalar(nmr[:, :], nmr[:, :], -1.0, 0.0, ALU.mult, ALU.add))

        def write_normed(e, x):
            if x["n"] >= 1:
                old = norms[x["n"] - 1]
                e.wait_ge(filled, find(f"turn{old['m'] + 1}", old["b"], KT - 1)["n"] + 1)
            for t in range(TT):
                ins = e.tensor_scalar(NRM[:, t, :], X[:, x["b"] * TT + t, :], rs[:, t:t + 1], nmr[:, t:t + 1],
                                      ALU.mult, ALU.add)
            ins.then_inc(normed[x["eng"]], 1)

        norms = [a[0] for k, a in plan if k == "ln"]
        divisions = [a[0] for k, a in plan if k == "divide"]

        def wait_normed(e, m, b):
            x = next(x for x in norms if (x["m"], x["b"]) == (m, b))
            e.wait_ge(normed[x["eng"]], x["count"])

        def wait_lo(e, f):
            e.wait_ge(split[f["lo"]], f["lo_count"])

        def wait_division(e, sems, upto):
            for eng in sems:
                done = [x["count"] for x in divisions[:upto] if x["eng"] == eng]
                if done:
                    e.wait_ge(sems[eng], done[-1])

        res_order = [(k, a[0]) for k, a in plan if k in ("residual1", "residual2")]
        block = ctx.enter_context(nc.Block())

        @block.sync
        def _(sp):
            for kind, a in plan:
                if kind == "setup":
                    xv = x.rearrange("b (t p) c -> b p t c", p=P)
                    av = w_ada.rearrange("(k p) n -> p k n", p=P)
                    sp.dma_start(X[:, 0:TT, :], xv[0]).then_inc(x_in[0], 16)
                    sp.dma_start(PC[:, :], cols).then_inc(cols_in, 16)
                    sp.dma_start(w_adaraw[:, :, 0:2 * C], av[:, :, 0:2 * C]).then_inc(ada0_in, 16)
                    sp.dma_start(w_qraw, w_qkv.rearrange("(k p) n -> p k n", p=P)).then_inc(wq_in, 16)
                    sp.dma_start(RW[:, :, :].rearrange("p r c -> p (r c)"),
                                 rows.broadcast_to([P, 4 * C])).then_inc(rows_in, 16)
                    sp.wait_ge(consts, 3)
                    for half in range(2):
                        sp.dma_start(KA[64 * half + QROWS:64 * half + QROWS + MROWS, :, :].bitcast(F32),
                                     MR[0:MROWS, :].bitcast(F32).unsqueeze(1).broadcast_to([MROWS, H // 2, N])
                                     ).then_inc(ones_in, 16)
                    sp.dma_start(TR[:, :, :].rearrange("p r c -> p (r c)"),
                                 trows.broadcast_to([P, 5 * C])).then_inc(trows_in, 16)
                    sp.dma_start(w_adaraw[:, :, 2 * C:6 * C], av[:, :, 2 * C:6 * C]).then_inc(ada1_in, 16)
                    for b in range(1, B):
                        sp.dma_start(X[:, b * TT:(b + 1) * TT, :], xv[b]).then_inc(x_in[b], 16)
                    sp.dma_start(w_praw[:, :, :], w_proj.rearrange("(k p) n -> p k n", p=P)).then_inc(wp_in, 16)
                if kind == "load_mlp":
                    sp.wait_ge(filled, find("ada", 1)["n"] + 1)
                    sp.wait_ge(filled, find("gate", B - 1, 1)["n"] + 1)
                    sp.dma_start(w_1raw[:, :, :], w_fc1.rearrange("(k p) n -> p k n", p=P)).then_inc(w1_in, 16)
                    sp.dma_start(w_2raw[:, :, :], w_fc2.rearrange("(k p) n -> p k n", p=P)).then_inc(w2_in, 16)
                if kind == "qk_rows":
                    b, mt = a
                    if b >= 1:
                        sp.wait_ge(scored, 2 * ((b - 1) * G * TT + (8 if mt == 0 else 16)))
                    for dst, which, parts in ((QA, 0, (0, 0, 1)), (KA, 1, (0, 1, 0))):
                        wait_lo(sp, find("qk", b, which, mt))
                        for half in range(2):
                            for blk, hl in enumerate(parts):
                                sp.dma_start(
                                    dst[64 * half + D * blk:64 * half + D * (blk + 1), 4 * mt:4 * mt + 4, :].bitcast(F32),
                                    QK[64 * half:64 * half + 64, which, hl, :].bitcast(F32)).then_inc(qk_in[mt], 16)
                if kind == "fill" and a[0]["kind"] == "maxrow":
                    b, g = a[0]["args"]
                    sp.wait_ge(rel["act"], a[0]["count"])
                    for half in range(2):
                        sp.dma_start(QA[64 * half + QROWS:64 * half + QROWS + MROWS, 2 * g:2 * g + 2, :].bitcast(F32),
                                     MR[4 * half:4 * half + 4, :].bitcast(F32)).then_inc(mrow_in[g % 2], 16)
                if kind == "attn_out":
                    n = a[0]
                    b, g = divmod(n, G)
                    sp.wait_ge(o_copied, n + 1)
                    if g in (0, 2) and b >= 1:
                        last_use = (b - 1) * 4 + (4 if g else 2)
                        wait_division(sp, attn_split, last_use)
                        wait_division(sp, attn_full, last_use)
                    part = slice(64 * (g % 2), 64 * (g % 2) + 64)
                    sp.dma_start(OC[part, g // 2, :], OS[0:P:2, :]).then_inc(o_in, 16)
                    sp.dma_start(LC[part, g // 2, :], OS[1:P:2, :]).then_inc(o_in, 16)
                if kind == "fill" and a[0]["kind"] == "fc2":
                    b, t = a[0]["args"]
                    k = b * TT + t
                    sp.wait_ge(y_ready, k + 1)
                    sp.dma_start(out[b, t * P:(t + 1) * P, :], X[:, k, :]).then_inc(y_out, 16)
            sp.wait_ge(y_out, 16 * NT)

        @block.tensor
        def _(pe):
            def products(psum, left, right, tiles, lo, hi):
                parts = ((0, 0), (1, 0), (0, 1))
                mm = None
                for k in range(tiles):
                    for i, (l, r) in enumerate(parts):
                        if lo <= 3 * k + i < hi:
                            mm = pe.matmul(psum, left(l, k), right(r, k), start=(k == 0 and i == 0),
                                           stop=(k == tiles - 1 and i == 2))
                return mm

            for kind, a in plan:
                if kind == "part" or kind == "fill" and not a[0]["parted"]:
                    if kind == "part":
                        what, args, number, lo, hi = a
                        last_part = hi == MATMULS[what]
                    else:
                        what, args, number, lo = a[0]["kind"], a[0]["args"], a[0]["n"], 0
                        hi, last_part = MATMULS.get(what), True
                    if number >= RING and lo == 0:
                        old = fills[number - RING]
                        pe.wait_ge(rel[old["eng"]], old["count"])
                    ps = SM[number % RING]
                    if what == "ada":
                        pe.wait_ge(silu_ready, 1)
                        pe.wait_ge((ada0_in, ada1_in)[args[0]], 16)
                        first = SH_MLP if args[0] else SH_MSA
                        for c in range(2 * KT):
                            for k in range(KT):
                                mm = pe.matmul(ps[:, B * c:B * c + B],
                                               w_adaraw[:, k, first * C + c * P:first * C + (c + 1) * P],
                                               silu[:, k * B:(k + 1) * B], start=(k == 0), stop=(k == KT - 1))
                    elif what == "gate":
                        b, m = args
                        pe.wait_ge(silu_ready, 2)
                        pe.wait_ge(ada1_in, 16)
                        c0 = (G_MLP if m else G_MSA) * C
                        for k in range(KT):
                            mm = pe.matmul(ps[:, 0:C], silu_wide[:, k, b, :], w_adaraw[:, k, c0:c0 + C],
                                           start=(k == 0), stop=(k == KT - 1))
                    elif what in ("turn1", "turn2"):
                        b, k = args
                        pe.wait_ge(consts, 2)
                        wait_normed(pe, int(what[-1]) - 1, b)
                        for t in range(TT):
                            mm = pe.transpose(ps[:, t * P:(t + 1) * P], NRM[:, t, k * P:(k + 1) * P], ident[:, :])
                    elif what == "qk":
                        b, which, mt = args
                        pe.wait_ge(wq_split, 1)
                        for k in range(KT):
                            wait_lo(pe, find("turn1", b, k))
                        c0 = which * C + mt * P
                        mm = products(ps[:, :], lambda l, k: (wqkv_h, wqkv_l)[l][:, k, c0:c0 + P],
                                      lambda r, k: HT[:, r, k, :], KT, lo, hi)
                    elif what == "v":
                        b, t = args
                        pe.wait_ge(wq_split, 1)
                        for k in range(KT):
                            wait_lo(pe, find("turn1", b, k))
                        mm = products(ps[:, 0:C], lambda l, k: HT[:, l, k, t * P:(t + 1) * P],
                                      lambda r, k: (wqkv_h, wqkv_l)[r][:, k, 2 * C:3 * C], KT, lo, hi)
                    elif what == "max":
                        b, g, j, t = args
                        h = g * GH + j
                        if (g % 2, j, t) == (0, 0, 0):
                            pe.wait_ge(qk_in[g // 2], 16 * 12 * (b + 1))
                        r = half_rows(h)
                        mm = pe.matmul(ps[:, :], QA[r:r + QROWS, h // 2, t * P:(t + 1) * P],
                                       KA[r:r + QROWS, h // 2, :], start=True, stop=True)
                    elif what == "maxrow":
                        b, g = args
                        pe.wait_ge(maxed, b * G + g + 1)
                        for t in range(TT):
                            mm = pe.transpose(ps[0:2 * GH, t * P:(t + 1) * P], ms[:, t, :].bitcast(F32), ident[:, :])
                    elif what == "proj":
                        b, t = args
                        wait_division(pe, attn_split, 4 * b + 3 + t // 2)
                        pe.wait_ge(w_split, 1)
                        mm = products(ps[:, 0:C], lambda l, k: AH[:, l, k, t * P:(t + 1) * P],
                                      lambda r, k: (wp_h, wp_l)[r][:, k, :], KT, lo, hi)
                    elif what == "fc1":
                        b, half, i = args
                        for k in range(KT):
                            wait_lo(pe, find("turn2", b, k))
                        pe.wait_ge(w_split, 3)
                        for e in range(lo // (3 * KT), hi // (3 * KT)):
                            c0 = (2 * i + e) * P
                            mm = products(ps[:, e * HALF:(e + 1) * HALF], lambda l, k: (w1_h, w1_l)[l][:, k, c0:c0 + P],
                                          lambda r, k: AH[:, r, k, half * HALF:(half + 1) * HALF],
                                          KT, 0, 3 * KT)
                    elif what == "fc2":
                        b, t = args
                        pe.wait_ge(w_split, 5)
                        for i in range(FN // 2):
                            wait_gelu(pe, find("fc1", b, t // 2, i))
                        c0, u = (t % 2) * P, gelu_output(b, t // 2)
                        mm = products(ps[:, 0:C], lambda l, k: u[:, l, k, c0:c0 + P],
                                      lambda r, k: (w2_h, w2_l)[r][:, k, :], FN, lo, hi)
                    if last_part:
                        mm.then_inc(filled, 1)
                if kind == "scores":
                    s, half = a
                    b, i = divmod(s, G * TT)
                    g, kt = divmod(i, TT)
                    n = s // TT
                    if s >= 1:
                        pe.wait_ge(exped, 2 * (s - 1) + half + 1)
                    if kt == 0 and half == 0:
                        pe.wait_ge(mrow_in[g % 2], 32 * (n // 2 + 1))
                        if n == 0:
                            pe.wait_ge(ones_in, 32)
                    for e in range(2):
                        h = g * GH + 2 * half + e
                        r = half_rows(h)
                        mm = pe.matmul(ST[half][:, e, :], KA[r:r + QROWS + MROWS, h // 2, kt * P:(kt + 1) * P],
                                       QA[r:r + QROWS + MROWS, h // 2, :], start=True, stop=True)
                    mm.then_inc(scored, 1)
                if kind == "values":
                    s = a[0]
                    b, i = divmod(s, G * TT)
                    g, kt = divmod(i, TT)
                    n = s // TT
                    pe.wait_ge(exped, 2 * s + 2)
                    if i == 0:
                        pe.wait_ge(v_ready, TT * (b + 1))
                    if kt == 0 and n >= 1:
                        pe.wait_ge(o_copied, n)
                    for j in range(GH):
                        mm = pe.matmul(O[2 * D * j:2 * D * (j + 1), :], VA[:, kt, g * GH + j, :],
                                       PB[:, s % 2, j, :], start=(kt == 0), stop=(kt == TT - 1))
                    mm.then_inc(valued, 1)

        @block.scalar
        def _(act):
            for kind, a in plan:
                if kind == "setup":
                    act.wait_ge(cols_in, 16)
                    act.activation(tnh[:, :], col("cond", 0, 2 * B), ACT.Tanh, scale=0.5).then_inc(tanh_c, 1)
                    act.wait_ge(wq_in, 16)
                    act.activation(wqkv_h[:, :, :], w_qraw, ACT.Copy).then_inc(wq_hi, 1)
                if kind == "fill" and a[0]["eng"] == "act":
                    f = a[0]
                    what, args, ps = f["kind"], f["args"], SM[f["slot"]]
                    act.wait_ge(filled, f["n"] + 1)
                    if what in ("turn1", "turn2", "qk"):
                        if f["split"] >= 2:
                            wait_lo(act, next(x for x in fills if x.get("split") == f["split"] - 2))
                        if what == "qk":
                            b, which, mt = args
                            if mt == 1:
                                act.wait_ge(qk_in[0], 16 * 12 * (b + 1))
                            elif b >= 1:
                                act.wait_ge(qk_in[1], 16 * 12 * b)
                            act.wait_ge(silu_ready, 1)
                            i = 2 * which + mt
                            dst, bias, scale = QK[:, which, 0, :], qkb[:, i:i + 1], qkg[:, i:i + 1]
                        else:
                            b, k = args
                            m = int(what[-1]) - 1
                            act.wait_ge(affine, m + 1)
                            dst = (HT, AH)[m][:, 0, k, :]
                            bias, scale = LB[:, m, k, b:b + 1], LA[:, m, k, b:b + 1]
                        act.activation(FULL[:, f["split"] % 2, :], ps[:, :], ACT.Identity, bias=bias, scale=scale)
                        act.activation(dst, ps[:, :], ACT.Identity, bias=bias, scale=scale).then_inc(rel["act"], 1)
                    elif what == "maxrow":
                        b, g = args
                        n = b * G + g
                        if n >= 1:
                            act.wait_ge(mrow_in[(g - 1) % 2], 32 * ((n - 1) // 2 + 1))
                        else:
                            act.wait_ge(ones_in, 32)
                        act.activation(MR[:, :], ps[0:2 * GH, :], ACT.Copy).then_inc(rel["act"], 1)
                    elif what == "fc1":
                        b, half, i = args
                        q = f["gelu"]
                        for x in reversed(fills[:f["n"]]):
                            if x.get("buffer") == f["buffer"]:
                                wait_gelu(act, x)
                                break
                        if b == B - 1:
                            act.wait_ge(valued, STEPS)
                        for func, dst in zip((ACT.Identity, ACT.Square), gelu_buffers(f)):
                            for e in range(2):
                                mm = act.activation(dst[:, e, :], ps[:, e * HALF:(e + 1) * HALF], func,
                                                    bias=col("fc1_b", 2 * i + e))
                        mm.then_inc(rel["act"], 1)
                if kind == "gelu_c":
                    q = a[0]["gelu"]
                    act.wait_ge(g_mid, q + 1)
                    vg = gelu_buffers(a[0])[1]
                    act.activation(vg, vg, ACT.Tanh,
                                   scale=GELU_SCALE * GELU_CUBIC).then_inc(g_tanh, 1)
                if kind == "scores":
                    s, half = a
                    act.wait_ge(scored, 2 * s + half + 1)
                    if s == 1:
                        act.wait_ge(wq_split, 1)
                    if s >= 2:
                        act.wait_ge(valued, s - 1)
                    act.activation(PB[:, s % 2, 2 * half:2 * half + 2, :], ST[half][:, :, :],
                                   ACT.Exp).then_inc(exped, 1)
                if kind == "attn_out":
                    n = a[0]
                    act.wait_ge(valued, TT * (n + 1))
                    if n >= 1:
                        act.wait_ge(o_in, 32 * n)
                    act.activation(OS[:, :], O[:, :], ACT.Copy).then_inc(o_copied, 1)
                if kind == "weights":
                    i = a[0]
                    act.wait_ge((wp_in, w1_in, w1_in, w2_in, w2_in)[i], 16)
                    raw, h, _l = weight_parts(i)
                    act.activation(h, raw, ACT.Copy).then_inc(w_hi, 1)
                if kind == "attn_hi":
                    x = a[0]
                    b, T, cs = x["b"], x["T"], slice(x["c"] * HALF, (x["c"] + 1) * HALF)
                    act.wait_ge(attn_full[x["eng"]], x["count"])
                    if b >= 1:
                        act.wait_ge(filled, find("fc1", b - 1, 1, 3)["n"] + 1)
                    act.activation(AH[:, 0, T, cs], OC[:, T, cs], ACT.Copy).then_inc(attn_hi, 1)

        @block.vector
        def _(dve):
            done = [0]
            seen_aggr = [0]

            def link(ins):
                done[0] += 1
                ins.then_inc(dve_seq, 1)
                dve.wait_ge(dve_seq, done[0])

            def take(f):
                dve.wait_ge(filled, f["n"] + 1)
                return SM[f["slot"]]

            for kind, a in plan:
                if kind == "setup":
                    dve.wait_ge(cols_in, 16)
                    dve.wait_ge(tanh_c, 1)
                    link(dve.scalar_tensor_tensor(out=silu[:, :], in0=tnh[:, :], scalar=1.0,
                                                  in1=col("cond", 0, 2 * B), op0=ALU.add, op1=ALU.mult))
                    dve.tensor_scalar(qkg[:, 0:2], col("qk_g", 0, 2), float(D) ** -0.5, None, ALU.mult)
                    dve.tensor_copy(qkg[:, 2:4], col("qk_g", 2, 2))
                    dve.tensor_scalar(adab1[:, :], col("ada_b", 0, 12), 1.0, None, ALU.add)
                    link(dve.tensor_scalar(silu[:, :], silu[:, :], 0.5, None, ALU.mult))
                    dve.tensor_tensor(qkb[:, :], col("qk_b", 0, 4), qkg[:, :], ALU.mult).then_inc(silu_ready, 1)
                if kind == "fill" and a[0]["eng"] == "dve":
                    f = a[0]
                    what, args = f["kind"], f["args"]
                    ps = take(f)
                    if what == "ada":
                        m = args[0]
                        sh, sc = ((SH_MSA, SC_MSA), (SH_MLP, SC_MLP))[m]
                        w, bb = ("ln1_w", "ln1_b") if m == 0 else ("ln2_w", "ln2_b")
                        for k in range(KT):
                            p_sh, p_sc = ps[:, B * k:B * k + B], ps[:, B * (KT + k):B * (KT + k) + B]
                            one = adab1[:, sc * KT + k:sc * KT + k + 1]
                            dve.tensor_scalar(LA[:, m, k, :], p_sc, one, col(w, k), ALU.add, ALU.mult)
                            link(dve.tensor_scalar(lt[:, k, :], p_sc, one, col(bb, k), ALU.add, ALU.mult))
                            link(dve.scalar_tensor_tensor(out=LB[:, m, k, :], in0=p_sh, scalar=col("ada_b", sh * KT + k),
                                                          in1=lt[:, k, :], op0=ALU.add, op1=ALU.add))
                        dve.tensor_copy(lt[:, :, :], LA[:, m, :, :]).then_inc(affine, 1)
                        dve.wait_ge(affine, m + 1)
                        dve.tensor_copy(lt[:, :, :], LA[:, m, :, :]).then_inc(rel["dve"], 1)
                    elif what == "gate":
                        b, m = args
                        dve.wait_ge(trows_in, 16)
                        dve.tensor_tensor(GATE[:, b, m, :], ps[:, 0:C], TR[:, TROW_AMLP if m else TROW_AMSA, :],
                                          ALU.add).then_inc(rel["dve"], 1)
                    elif what == "v":
                        b, t = args
                        k = b * TT + t
                        dve.wait_ge(rows_in, 16)
                        if b >= 1:
                            dve.wait_ge(v_ready, TT * b)
                        dve.tensor_tensor(VT[:, t, :], ps[:, 0:C], RW[:, ROW_BV, :], ALU.add).then_inc(rel["dve"], 1)
                    elif what == "max":
                        b, g, j, t = args
                        n = b * G + g
                        if (j, t) == (0, 0) and n >= 1:
                            dve.wait_ge(maxed, n)
                        pos = 2 * (j % 2) + j // 2
                        dve.tensor_reduce(nm[:, t, pos:pos + 1], ps[:, :], AX.X, ALU.max,
                                          negate=True).then_inc(rel["dve"], 1)
                        if (j, t) == (GH - 1, TT - 1):
                            dve.wait_ge(rel["dve"], f["count"])
                            if n >= 1:
                                dve.wait_ge(filled, find("maxrow", *divmod(n - 1, G))["n"] + 1)
                            nmv = nm[:, :, :].rearrange("p t (a l) -> p t a l", a=2)
                            msv = ms[:, :, :].rearrange("p t (a s l) -> p t a s l", a=2, s=2)
                            for half in range(2):
                                ins = dve.tensor_copy(msv[:, :, half, 0, :], nmv[:, :, half, :])
                            link(ins)
                            for half in range(2):
                                ins = dve.tensor_tensor(msv[:, :, half, 1, :], nmv[:, :, half, :],
                                                        msv[:, :, half, 0, :].bitcast(F32), ALU.subtract)
                            ins.then_inc(maxed, 1)
                    elif what == "proj":
                        b, t = args
                        dve.wait_ge(gate_ready, 2 * B)
                        dve.wait_ge(biased, res_order.index(("residual1", b)) + 1)
                        xt = X[:, b * TT + t, :]
                        if t >= 1:
                            dve.wait_ge(x2_ready, b * TT + t)
                        elif b >= 1:
                            dve.wait_ge(y_ready, b * TT)
                        dve.tensor_tensor(PT[:, :], ps[:, 0:C], GATE[:, b, 0, :], ALU.mult).then_inc(rel["dve"], 1)
                        dve.wait_ge(rel["dve"], f["count"])
                        dve.tensor_tensor(xt, PT[:, :], xt, ALU.add).then_inc(x2_ready, 1)
                    elif what == "fc2":
                        b, t = args
                        k = b * TT + t
                        dve.wait_ge(biased, res_order.index(("residual2", b)) + 1)
                        if t == 0:
                            dve.wait_ge(x2_ready, (b + 1) * TT)
                        else:
                            dve.wait_ge(y_ready, k)
                        dve.tensor_tensor(PT[:, :], ps[:, 0:C], GATE[:, b, 1, :], ALU.mult).then_inc(rel["dve"], 1)
                        dve.wait_ge(rel["dve"], f["count"])
                        dve.tensor_tensor(X[:, k, :], PT[:, :], X[:, k, :], ALU.add).then_inc(y_ready, 1)
                if kind == "gelu_b":
                    f = a[0]
                    q = f["gelu"]
                    dve.wait_ge(rel["act"], f["count"])
                    xg, vg = gelu_buffers(f)
                    dve.scalar_tensor_tensor(out=vg, in0=vg, scalar=1.0 / GELU_CUBIC, in1=xg,
                                             op0=ALU.add, op1=ALU.mult).then_inc(g_mid, 1)
                if kind == "gelu_d":
                    f = a[0]
                    q = f["gelu"]
                    b, half, i = f["args"]
                    xg, vg = gelu_buffers(f)
                    dve.wait_ge(g_tanh, q + 1)
                    link(dve.scalar_tensor_tensor(out=vg, in0=vg, scalar=1.0, in1=xg, op0=ALU.add, op1=ALU.mult))
                    if (b, half) == (B - 1, 1):
                        dve.wait_ge(scored, 2 * STEPS)
                    elif i == 0 and (b, half) != (0, 0):
                        b0, h0 = (b, 0) if half else (b - 1, 1)
                        dve.wait_ge(filled, find("fc2", b0, 2 * h0 + 1)["n"] + 1)
                    if q == 0:
                        dve.wait_ge(w_split, 5)
                        dve.wait_ge(w_hi, 5)
                    dve.tensor_copy(gelu_output(b, half)[:, 0, 2 * i:2 * i + 2, :], vg).then_inc(g_full, 1)
                if kind == "gelu_lo" and a[0]["ulo"] == "dve":
                    write_gelu_lo(dve, a[0])
                if kind == "silu_wide":
                    dve.wait_ge(consts, 2)
                    for k in range(KT):
                        for b in range(B):
                            mm = dve.tensor_scalar(silu_wide[:, k, b, :], ident[:, :], 0.0,
                                                   silu[:, k * B + b:k * B + b + 1], ALU.mult, ALU.add)
                    mm.then_inc(silu_ready, 1)
                if kind == "wq_lo":
                    dve.wait_ge(wq_hi, 1)
                    dve.wait_ge(wq_in, 16)
                    dve.tensor_tensor(wqkv_l[:, :, :], w_qraw, wqkv_h[:, :, :].bitcast(F32),
                                      ALU.subtract).then_inc(wq_split, 1)
                if kind == "lo":
                    f = a[0]
                    dve.wait_ge(rel["act"], f["count"])
                    h, l = split_tile(f)
                    dve.tensor_tensor(l, FULL[:, f["split"] % 2, :], h.bitcast(F32),
                                      ALU.subtract).then_inc(split["dve"], 1)
                if kind == "stats":
                    m, b, t = a
                    if m == 0:
                        dve.wait_ge(x_in[b], 16)
                    else:
                        dve.wait_ge(x2_ready, TT * b + t + 1)
                    if seen_aggr[0]:
                        dve.wait_ge(aggregated, seen_aggr[0])
                    dve.bn_stats(st6[:, t, :], X[:, b * TT + t, :]).then_inc(stats_done, 1)
                if kind == "ln":
                    x = a[0]
                    dve.wait_ge(stats_done, TT * (x["n"] + 1))
                    for e in range(x["n"]):
                        if e == x["n"] - 1:
                            dve.wait_ge(normed[norms[e]["eng"]], norms[e]["count"])
                    for t in range(TT):
                        ins = dve.bn_aggr(mv[:, t, :], st6[:, t, :])
                    ins.then_inc(aggregated, 1)
                    seen_aggr[0] += 1
                    dve.wait_ge(aggregated, seen_aggr[0])
                    link(dve.tensor_scalar(ve[:, :], mv[:, :, 1], EPS, None, ALU.add))
                    ins = dve.tensor_scalar(rs[:, :].bitcast(I32), ve[:, :].bitcast(I32), -0.5, RSQRT_SEED,
                                            ALU.mult, ALU.add)
                    if x["eng"] == "pool":
                        ins.then_inc(seeded, 1)
                    else:
                        link(ins)
                        newton(dve, link)
                        write_normed(dve, x)
                if kind == "recip":
                    b, T, c = a
                    dve.wait_ge(o_in, 32 * (G * b + 2 * T + 2))
                    cs = slice(c * HALF, (c + 1) * HALF)
                    dve.reciprocal(LC[:, T, cs], LC[:, T, cs]).then_inc(recip, 1)
                if kind == "divide" and a[0]["eng"] == "dve":
                    divide(dve, a[0])
                if kind == "attn_lo" and a[0]["eng"] == "dve":
                    divide_lo(dve, a[0])

        @block.gpsimd
        def _(pool):
            seq = [0]

            def link(ins):
                seq[0] += 1
                ins.then_inc(pool_seq, 1)
                pool.wait_ge(pool_seq, seq[0])

            def lo(dst, full, hi):
                return pool.tensor_tensor(dst, full, hi.bitcast(F32), ALU.subtract)

            for kind, a in plan:
                if kind == "setup":
                    pool.memset(ident[:, :], 0.0).then_inc(consts, 1)
                    pool.wait_ge(consts, 1)
                    pool.affine_select(out=ident[:, :], in_=ident[:, :], compare_op=ALU.not_equal, fill=1.0,
                                       base=0, pattern=[[-1, P]], channel_multiplier=1).then_inc(consts, 1)
                    pool.memset(MR[:, :].bitcast(F32), 1.0).then_inc(consts, 1)
                    pool.memset(VA[:, :, :, :], 1.0).then_inc(pool_seq, 1)
                    seq[0] += 1
                    pool.wait_ge(pool_seq, seq[0])
                if kind == "ln" and a[0]["eng"] == "pool":
                    pool.wait_ge(seeded, a[0]["count"])
                    newton(pool, link)
                    write_normed(pool, a[0])
                if kind == "residual1" or kind == "residual2":
                    b, m = a[0], int(kind[-1]) - 1
                    wait_normed(pool, m, b)
                    pool.wait_ge(gate_ready, 2 * b + m + 1)
                    at = res_order.index((kind, b))
                    if at >= 1:
                        pool.wait_ge(biased, at)
                    link(pool.tensor_tensor(GB[:, :], GATE[:, b, m, :], RW[:, ROW_B2 if m else ROW_BP, :], ALU.mult))
                    for t in range(TT):
                        ins = pool.tensor_tensor(X[:, b * TT + t, :], X[:, b * TT + t, :], GB[:, :], ALU.add)
                    ins.then_inc(biased, 1)
                if kind == "weights":
                    pool.wait_ge(w_hi, a[0] + 1)
                    raw, h, l = weight_parts(a[0])
                    lo(l, raw, h).then_inc(w_split, 1)
                if kind == "fill":
                    f = a[0]
                    what, args = f["kind"], f["args"]
                    if f.get("lo") == "pool":
                        pool.wait_ge(rel["act"], f["count"])
                        h, l = split_tile(f)
                        lo(l, FULL[:, f["split"] % 2, :], h).then_inc(split["pool"], 1)
                    if what == "gate":
                        b, m = args
                        if (b, m) == (0, 0):
                            pool.wait_ge(trows_in, 16)
                            pool.wait_ge(rows_in, 16)
                            link(pool.tensor_tensor(TR[:, TROW_G1, :], TR[:, TROW_G1, :], TR[:, TROW_GO, :], ALU.mult))
                            link(pool.tensor_scalar(TR[:, TROW_G2, :], TR[:, TROW_G2, :], 0.5, 1.0, ALU.mult, ALU.mult))
                            link(pool.tensor_scalar(RW[:, ROW_B2, :], RW[:, ROW_B2, :], 2.0, 1.0, ALU.mult, ALU.mult))
                        pool.wait_ge(rel["dve"], f["count"])
                        pool.tensor_tensor(GATE[:, b, m, :], GATE[:, b, m, :], TR[:, TROW_G2 if m else TROW_G1, :],
                                           ALU.mult).then_inc(gate_ready, 1)
                if kind == "v_place":
                    b = a[0]
                    pool.wait_ge(rows_in, 16)
                    if b >= 1:
                        pool.wait_ge(valued, G * TT * b)
                    for t in range(TT):
                        pool.wait_ge(rel["dve"], find("v", b, t)["count"])
                        pool.tensor_tensor(VA[:, t, :, 0:2 * D:2],
                                           VT[:, t, :].rearrange("p (h d) -> p h d", h=H),
                                           RW[:, ROW_GV, :].rearrange("p (h d) -> p h d", h=H),
                                           ALU.mult).then_inc(v_ready, 1)
                if kind == "gelu_lo" and a[0]["ulo"] == "pool":
                    write_gelu_lo(pool, a[0])
                if kind == "divide" and a[0]["eng"] == "pool":
                    divide(pool, a[0])
                if kind == "attn_lo" and a[0]["eng"] == "pool":
                    divide_lo(pool, a[0])


def kernel(x, cond_1024, L0_cond_ln1_w, L0_cond_ln1_b, L0_cond_ln2_w, L0_cond_ln2_b, L0_cond_gamma_qkv,
           L0_cond_gamma_attn_out, L0_cond_w_qkv, L0_cond_b_qkv, L0_cond_w_proj, L0_cond_b_proj, L0_cond_w_fc1,
           L0_cond_b_fc1, L0_cond_w_fc2, L0_cond_b_fc2, L0_cond_w_ada, L0_cond_b_ada, L0_cond_gamma1,
           L0_cond_gamma2):
    import numpy as np
    import concourse.bacc as bacc
    from concourse.bass_utils import run_bass_kernel_spmd as run

    def spread(w):
        w = np.asarray(w)
        lead = w.shape[:-1]
        w = w.reshape(*lead, KT, 4, 2, D)
        return np.moveaxis(w, -3, -1).reshape(*lead, C)

    def tiles(v):
        return np.asarray(v).reshape(-1, P).T

    w_qkv, b_qkv, g_qkv = (np.asarray(v) for v in (L0_cond_w_qkv, L0_cond_b_qkv, L0_cond_gamma_qkv))
    w = np.concatenate([spread(w_qkv[:, 0:C]), spread(w_qkv[:, C:2 * C]), w_qkv[:, 2 * C:]], axis=1)
    qk = [np.concatenate([spread(v[0:C]), spread(v[C:2 * C])]) for v in (b_qkv, g_qkv)]
    cond = np.asarray(cond_1024).reshape(B, KT, P).transpose(2, 1, 0).reshape(P, KT * B)
    cols = np.concatenate([tiles(qk[0]), tiles(qk[1]), tiles(L0_cond_ln1_w), tiles(L0_cond_ln1_b),
                           tiles(L0_cond_ln2_w), tiles(L0_cond_ln2_b), tiles(L0_cond_b_fc1),
                           tiles(L0_cond_b_ada), cond], axis=1)
    b_ada = np.asarray(L0_cond_b_ada).reshape(6, C)
    rows = np.concatenate([b_qkv[2 * C:], g_qkv[2 * C:], np.asarray(L0_cond_b_proj), np.asarray(L0_cond_b_fc2)])
    trows = np.concatenate([np.asarray(L0_cond_gamma1), np.asarray(L0_cond_gamma_attn_out),
                            np.asarray(L0_cond_gamma2), b_ada[G_MSA], b_ada[G_MLP]])
    w_ada = np.asarray(L0_cond_w_ada)
    arrays = {"x": np.asarray(x), "cols": cols, "rows": rows[None, :], "trows": trows[None, :], "w_qkv": w,
              "w_proj": np.asarray(L0_cond_w_proj), "w_fc1": np.asarray(L0_cond_w_fc1),
              "w_fc2": np.asarray(L0_cond_w_fc2), "w_ada": w_ada}
    nc = bacc.Bacc("TRN2", target_bir_lowering=False, num_devices=1)
    arrays = {k: np.ascontiguousarray(v) for k, v in arrays.items()}
    ins = {k: nc.dram_tensor("in_" + k, v.shape, F32, kind="ExternalInput").ap() for k, v in arrays.items()}
    y = nc.dram_tensor("y", (B, N, C), F32, kind="ExternalOutput").ap()
    block_program(nc, out=y, **ins)
    r = run(nc, [{"in_" + k: v for k, v in arrays.items()}], core_ids=[0])
    return r.results[0]["y"]
```

```python
from contextlib import ExitStack

import concourse.bass as bass
from concourse import mybir

F32 = mybir.dt.float32
F32R = mybir.dt.float32r
I32 = mybir.dt.int32
ALU = mybir.AluOpType
ACT = mybir.ActivationFunctionType
AX = mybir.AxisListType

P = 128
B, N, C, H = 4, 512, 256, 16
D = C // H
MLP = 4 * C
KT = C // P
TT = N // P
NT = B * TT
G = 4
GH = H // G
FN = MLP // P
HALF = N // 2
STEPS = B * G * TT
RING = 4
SCORE_RING = 3
EPS = 1e-6
GELU_CUBIC = 0.044715
GELU_SCALE = 0.7978845608028654
RSQRT_SEED = 1597463007.0
QROWS, MROWS = 3 * D, 2

COLS = {}
for _name, _n in (("qk_b", 4), ("qk_g", 4), ("ln1_w", 2), ("ln1_b", 2), ("ln2_w", 2), ("ln2_b", 2),
                  ("fc1_b", FN), ("ada_b", 12), ("cond", 2 * B)):
    COLS[_name] = (sum(n for _, n in COLS.values()), _n)
NCOLS = sum(n for _, n in COLS.values())
ROW_BV, ROW_GV, ROW_BP, ROW_B2 = range(4)
TROW_G1, TROW_GO, TROW_G2, TROW_AMSA, TROW_AMLP = range(5)
SH_MSA, SC_MSA, G_MSA, SH_MLP, SC_MLP, G_MLP = range(6)


MATMULS = {"qk": 3 * KT, "v": 3 * KT, "proj": 3 * KT, "fc1": 6 * KT, "fc2": 3 * FN}

AHEAD = {
    "turn1": (1.02, 1.51),
    "v": (2.72, 2.91, 3.67, 3.73),
    "qk0": (4.75, 5.8),
    "qk1": (15.84, 16.67),
    "residual1": (2.83,),
    "qk_rows0": (9.82,),
    "qk_rows1": (18.97,),
}
STATS1, LN1 = (7.05, 8.42, 9.54, 9.91), 12.59
BEHIND = {
    "proj": (3.08, 3.18, 3.27, 3.32),
    "stats": (3.17, 3.4, 3.41, 3.48),
    "ln2": (3.77,),
    "turn2": (5.49, 5.6),
    "residual2": (7.5,),
    "fc1": (6.32, 7.4, 7.45, 8.43, 9.49, 11.16, 11.62, 12.64),
    "fc2": (9.69, 10.1, 14.79, 15.79),
}
GELU = (0.3, 0.39, 0.83)
FC2_PARTS, FC2_EVERY = 3, 0.08
RECIP = ((11.67, 12.79), (17.49, 18.14))
DIVIDE = ((12.6, 15.39), (18.06, 18.39))
ATTN_HI = ((13.89, 14.24), (17.4, 17.5))
ATTN_LO = ((12.59, 13.19), (13.96, 14.15))
GATES = (0.44, 1.14, 2.16, 2.37, 2.99, 3.51, 4.34, 5.13)
QK_0, TURN_0 = (-0.81, 0.12, 2.57), (0.6, 0.66)
ADA1, RESIDUAL_0, LOAD_MLP = 5.66, 9.36, 12.32
WEIGHTS = (6.9, 12.08, 14.45, 15.0, 15.39)
TAIL = {
    "proj": (2.37, 2.58, 3.11, 3.28),
    "ln2": (2.99, 3.94),
    "turn2": (3.37, 4.26),
    "residual2": (4.12,),
    "fc1": (3.8, 4.79, 5.38, 5.62, 6.19, 6.63, 8.29, 8.35),
    "fc2": (11.98, 12.09, 13.12, 14.78),
}
TAIL_GELU = (0.39, 0.74, 1.14)
SCORES, VALUES = (-0.08, -0.04, 0.14, 0.34), 0.64
MAXES, MAXROW = 2.85, 3.32


TAIL_DVE_LO = (B * FN - 1,)


def make_plan():
    plan, fills = [], []
    counts = {}

    def count(*key):
        counts[key] = counts.get(key, 0) + 1
        return counts[key]

    def do(kind, *args):
        plan.append((kind, args))

    def fill(kind, *args, lo="pool", part=0, parts=1):
        if parts > 1:
            m = MATMULS[kind]
            do("part", kind, args, len(fills), m * part // parts, m * (part + 1) // parts)
            if part < parts - 1:
                return None
        eng = "act" if kind in ("turn1", "turn2", "qk", "maxrow", "fc1") else "dve"
        f = {"kind": kind, "args": args, "n": len(fills), "slot": len(fills) % RING,
             "eng": eng, "count": count("took", eng), "parted": parts > 1}
        if kind in ("turn1", "turn2", "qk"):
            f["split"] = count("split") - 1
            f["lo"], f["lo_count"] = lo, count("lo", lo)
        if kind == "fc1":
            f["gelu"] = count("gelu") - 1
            f["ulo"] = "dve" if f["gelu"] in TAIL_DVE_LO else "pool"
            f["ulo_count"] = count("ulo", f["ulo"])
            f["buffer"] = f["gelu"] % 2 if args[0] < B - 1 else 2 + f["gelu"] % 4
        fills.append(f)
        plan.append(("fill", (f,)))
        return f

    def maxes(n):
        b, g = divmod(n, G)
        return [("max", b, g, j, t) for t in range(TT) for j in range(GH)]

    def stats(m, b, tiles):
        for t in tiles:
            do("stats", m, b, t)

    def norm_tokens(m, b, tiles, eng="pool"):
        do("ln", {"m": m, "b": b, "tiles": tiles, "n": count("ln") - 1, "eng": eng,
                  "count": count("ln", eng), "stats": counts.get("stats", 0) + len(tiles)})
        counts["stats"] = counts.get("stats", 0) + len(tiles)

    def division(b, T, c, eng="pool"):
        return {"b": b, "T": T, "c": c, "eng": eng, "count": count("division", eng),
                "n": count("division") - 1}

    do("setup")
    stats(0, 0, range(TT))
    norm_tokens(0, 0, range(TT), "dve")
    fill("ada", 0)
    fill("turn1", 0, 0)
    fill("turn1", 0, 1, lo="dve")
    do("wq_lo")
    do("lo", fills[-1])
    fill("qk", 0, 0, 0)
    fill("qk", 0, 1, 0, lo="dve")
    do("lo", fills[-1])
    do("qk_rows", 0, 0)
    for t in range(TT):
        fill("v", 0, t)
    do("v_place", 0)
    do("silu_wide")
    stats(0, 1, range(TT))
    norm_tokens(0, 1, range(TT))
    gates = [("gate", b, m) for b in range(B) for m in range(2)]
    for m in maxes(0):
        fill(*m)
    fill("maxrow", 0, 0)

    timed = []

    def at(position, kind, *args):
        timed.append((position, count("timed"), kind, args))

    for s in range(STEPS):
        b, i = divmod(s, G * TT)
        n, kt = divmod(s, TT)
        for j in range(GH):
            at(s + SCORES[j], "scores", s, j)
        if s >= 1:
            at(s + VALUES, "values", s - 1)
        if i == 0 and b >= 1:
            at(s + VALUES, "v_place", b)
        if kt == 0 and s >= 1:
            at(s + VALUES, "attn_out", n - 1)
        if kt == 0 and n + 1 < B * G:
            for k, m in enumerate(maxes(n + 1)):
                at(s + (k + 0.5) * MAXES / (GH * TT), *m)
            at(s + MAXROW, "maxrow", *divmod(n + 1, G))
    for b in range(B):
        t0 = b * G * TT
        nb, pb = b + 1, b - 1
        if nb < B:
            for k in range(KT):
                at(t0 + AHEAD["turn1"][k] if b else TURN_0[k], "turn1", nb, k)
            for t in range(TT):
                at(t0 + AHEAD["v"][t], "v", nb, t)
            for mt in range(2):
                for which in range(2):
                    at(t0 + AHEAD[f"qk{mt}"][which], "qk", nb, which, mt)
                at(t0 + AHEAD[f"qk_rows{mt}"][0], "qk_rows", nb, mt)
            at(t0 + AHEAD["residual1"][0], "residual1", nb)
        if nb + 1 < B:
            for t in range(TT):
                at(t0 + STATS1[t], "stats", 0, nb + 1, t)
            at(t0 + LN1, "norm_tokens", 0, nb + 1, range(TT))
        if b == 0:
            for which in range(2):
                at(QK_0[which], "qk", 0, which, 1)
            at(QK_0[2], "qk_rows", 0, 1)
            for k, g in enumerate(gates):
                at(GATES[k], *g)
            at(ADA1, "ada", 1)
            at(RESIDUAL_0, "residual1", 0)
            at(LOAD_MLP, "load_mlp")
            for k in range(5):
                at(WEIGHTS[k], "weights", k)
        for T in range(2):
            for c in range(2):
                if (b, T) < (B - 1, 1):
                    at(t0 + RECIP[T][c], "recip", b, T, c)
                    at(t0 + DIVIDE[T][c], "divide", b, T, c)
        if pb >= 0:
            for t in range(TT):
                at(t0 + BEHIND["proj"][t], "proj", pb, t)
                at(t0 + BEHIND["stats"][t], "stats", 1, pb, t)
                at(t0 + BEHIND["fc2"][t], "fc2", pb, t)
            at(t0 + BEHIND["ln2"][0], "norm_tokens", 1, pb, range(TT))
            for c in range(2):
                at(t0 + BEHIND["turn2"][c], "turn2", pb, c)
            at(t0 + BEHIND["residual2"][0], "residual2", pb)
            for k in range(FN):
                at(t0 + BEHIND["fc1"][k], "fc1", pb, k // 4, k % 4)

    last = B - 1
    for position, kind, *args in (
            (0.0, "values", STEPS - 1), (0.1, "attn_out", B * G - 1),
            (1.0, "recip", last, 1, 0), (1.1, "divide", last, 1, 0), (1.3, "recip", last, 1, 1),
            (1.7, "divide", last, 1, 1), (TAIL["residual2"][0], "residual2", last)):
        at(STEPS + position, kind, *args)
    for t in range(TT):
        at(STEPS + TAIL["proj"][t], "proj", last, t)
        at(STEPS + TAIL["proj"][t] + 0.01, "stats", 1, last, t)
        at(STEPS + TAIL["fc2"][t], "fc2", last, t)
    for c in range(2):
        at(STEPS + TAIL["ln2"][c], "norm_tokens", 1, last, range(2 * c, 2 * c + 2), "dve")
        at(STEPS + TAIL["turn2"][c], "turn2", last, c)
    for k in range(FN):
        at(STEPS + TAIL["fc1"][k], "fc1", last, k // 4, k % 4)

    opened, held = None, []
    while timed or held:
        if held and not opened:
            position, _, kind, args = held.pop(0)
        else:
            timed.sort()
            position, _, kind, args = timed.pop(0)
        is_fill = kind in ("turn1", "turn2", "qk", "v", "proj", "fc1", "fc2", "max", "maxrow", "gate", "ada")
        if opened and is_fill:
            held.append((position, 0, kind, args))
        elif kind == "norm_tokens":
            norm_tokens(*args)
        elif kind == "divide":
            b, T, c = args
            tail = (b, T) == (last, 1)
            x = division(*args, eng="dve" if tail else "pool")
            do("divide", x)
            at(position + 0.3 if tail else b * G * TT + ATTN_HI[T][c], "attn_hi", x)
            at(position + 0.5 if tail else b * G * TT + ATTN_LO[T][c], "attn_lo", x)
        elif kind == "fc2" and FC2_PARTS > 1 and args[0] < last:
            opened = args
            fill(kind, *args, part=0, parts=FC2_PARTS)
            for k in range(1, FC2_PARTS):
                at(position + k * FC2_EVERY, "more", kind, args, k)
        elif kind == "more":
            kind, args, k = args
            fill(kind, *args, part=k, parts=FC2_PARTS)
            if k == FC2_PARTS - 1:
                opened = None
        elif is_fill:
            tail_lo = "dve" if (kind, args[0]) == ("turn2", last) else "pool"
            f = fill(kind, *args, lo=tail_lo)
            if tail_lo == "dve":
                at(position + 0.1, "lo", f)
            if kind == "fc1":
                for k, name in enumerate(("gelu_b", "gelu_c", "gelu_d")):
                    at(position + (TAIL_GELU if args[0] == last else GELU)[k], name, f)
                at(position + (TAIL_GELU if args[0] == last else GELU)[2] + 0.02, "gelu_lo", f)
        else:
            do(kind, *args)
    return plan, fills


def block_program(nc, x, cols, rows, trows, w_qkv, w_proj, w_fc1, w_fc2, w_ada, out):
    plan, fills = make_plan()

    def find(kind, *args):
        for f in fills:
            if f["kind"] == kind and f["args"] == args:
                return f
        raise KeyError((kind, args))

    with ExitStack() as ctx:
        def sb(name, shape, dt=F32):
            return ctx.enter_context(nc.sbuf_tensor(name, shape, dt))

        def sem(name):
            return ctx.enter_context(nc.semaphore(name))

        X = sb("X", [P, NT, C])
        wqkv_h, wqkv_l = sb("wqkv_h", [P, KT, 3 * C], F32R), sb("wqkv_l", [P, KT, 3 * C], F32R)
        wp_h, wp_l = sb("wp_h", [P, KT, C], F32R), sb("wp_l", [P, KT, C], F32R)
        w1_h, w1_l = sb("w1_h", [P, KT, MLP], F32R), sb("w1_l", [P, KT, MLP], F32R)
        w2_h, w2_l = sb("w2_h", [P, FN, C], F32R), sb("w2_l", [P, FN, C], F32R)
        QA = sb("QA", [P, H // 2, N], F32R)
        KA = sb("KA", [P, H // 2, N], F32R)
        QK = sb("QK", [P, 2, 2, N], F32R)
        PB = sb("PB", [P, 2, GH, N])
        VA = sb("VA", [P, TT, H, 2 * D])
        HT = sb("HT", [P, 2, KT, N], F32R)
        AH = sb("AH", [P, 2, KT, N], F32R)
        FULL = sb("FULL", [P, 2, N])
        NRM = sb("NRM", [P, TT, C])
        OS = sb("OS", [P, N])
        OC = sb("OC", [P, KT, N])
        LC = sb("LC", [P, KT, N])
        RW = sb("RW", [P, 4, C])
        GATE = sb("GATE", [P, B, 2, C])
        GB = sb("GB", [P, C])
        XV = sb("XV", [P, 2, 2, 2, HALF])
        PB_halves = PB[:, :, :, :].rearrange("p s j n -> p (s j n)").rearrange("p (q a e n) -> p a q e n", q=4, a=2, e=2)
        XV_flat = XV[:, :, :, :, :].rearrange("p a q e n -> p (a q e n)")
        TR = XV_flat[:, 0:5 * C].rearrange("p (r c) -> p r c", r=5)
        w_praw = XV_flat[:, 5 * C:7 * C].rearrange("p (k c) -> p k c", k=KT)
        VT = sb("VT", [P, TT, C])
        PT = sb("PT", [P, C])
        ident = sb("ident", [P, P])
        MR = sb("MR", [2 * GH, N], F32R)
        nm = sb("nm", [P, TT, GH])
        ms = sb("ms", [P, TT, 2 * GH], F32R)
        PC = sb("PC", [P, NCOLS])
        qkb = sb("qkb", [P, 4])
        qkg = sb("qkg", [P, 4])
        adab1 = sb("adab1", [P, 12])
        silu = sb("silu", [P, 2 * B])
        tnh = sb("tnh", [P, 2 * B])
        LA = sb("LA", [P, 2, KT, B])
        LB = sb("LB", [P, 2, KT, B])
        lt = sb("lt", [P, KT, B])
        st6 = sb("st6", [P, TT, 6])
        mv = sb("mv", [P, TT, 2])
        ve = sb("ve", [P, TT])
        rs = sb("rs", [P, TT])
        rt = sb("rt", [P, TT])
        nmr = sb("nmr", [P, TT])
        with nc.sbuf_tensor("w_adaraw", [P, KT, 6 * C], F32) as w_adaraw, \
                nc.sbuf_tensor("silu_wide", [P, KT, B, P], F32) as silu_wide:
            pass
        with nc.sbuf_tensor("w_1raw", [P, KT, MLP], F32) as w_1raw, \
                nc.sbuf_tensor("w_2raw", [P, FN, C], F32) as w_2raw:
            pass
        U = sb("U", [P, 2, FN, HALF], F32R)
        U_last = QA[:, :, :].rearrange("p j n -> p (j n)").rearrange("p (l k n) -> p l k n", l=2, k=FN)
        w_qraw = PB[:, 1, :, :].rearrange("p j n -> p (j n)")[:, 0:KT * 3 * C].rearrange("p (k n) -> p k n", k=KT)

        ST = [ctx.enter_context(nc.psum_tensor(f"ST{i}", [P, N], F32)) for i in range(SCORE_RING)]
        SM = [ctx.enter_context(nc.psum_tensor(f"SM{i}", [P, N], F32)) for i in range(RING)]
        O = ctx.enter_context(nc.psum_tensor("O", [P, N], F32))

        cols_in, rows_in, trows_in, ada0_in, ada1_in = map(sem, ("cols_in", "rows_in", "trows_in", "ada0_in", "ada1_in"))
        wq_in, wp_in, w1_in, w2_in, ones_in = map(sem, ("wq_in", "wp_in", "w1_in", "w2_in", "ones_in"))
        x_in = [sem(f"x_in{b}") for b in range(B)]
        consts = sem("consts")
        pool_seq = sem("pool_seq")
        tanh_c = sem("tanh_c")
        dve_seq = sem("dve_seq")
        silu_ready = sem("silu_ready")
        wq_hi, wq_split = sem("wq_hi"), sem("wq_split")
        w_hi, w_split = sem("w_hi"), sem("w_split")
        filled = sem("filled")
        rel = {"act": sem("act_took"), "dve": sem("dve_took")}
        stats_done, aggregated = sem("stats_done"), sem("aggregated")
        affine = sem("affine")
        seeded = sem("seeded")
        normed = {"pool": sem("pool_normed"), "dve": sem("dve_normed")}
        split = {"pool": sem("pool_split"), "dve": sem("dve_split")}
        qk_in = [sem("qk_in0"), sem("qk_in1")]
        mrow_in = [sem("mrow_in0"), sem("mrow_in1")]
        maxed = sem("maxed")
        v_ready = sem("v_ready")
        scored, exped, valued = sem("scored"), sem("exped"), sem("valued")
        o_copied, o_in = sem("o_copied"), sem("o_in")
        recip, attn_hi = sem("recip"), sem("attn_hi")
        attn_full = {"pool": sem("pool_attn_full"), "dve": sem("dve_attn_full")}
        attn_split = {"pool": sem("pool_attn_split"), "dve": sem("dve_attn_split")}
        gate_ready = sem("gate_ready")
        biased = sem("biased")
        x2_ready = sem("x2_ready")
        g_mid, g_tanh, g_full = map(sem, ("g_mid", "g_tanh", "g_full"))
        u_ready = {"pool": sem("pool_u_ready"), "dve": sem("dve_u_ready")}
        y_ready, y_out = sem("y_ready"), sem("y_out")

        def col(name, i, n=1):
            return PC[:, COLS[name][0] + i:COLS[name][0] + i + n]

        def half_rows(h):
            return 64 * (h % 2)

        def weight_parts(i):
            if i == 0:
                return w_praw[:, :, :], wp_h[:, :, :], wp_l[:, :, :]
            if i in (1, 2):
                return w_1raw[:, i - 1, :], w1_h[:, i - 1, :], w1_l[:, i - 1, :]
            k = slice((i - 3) * FN // 2, (i - 2) * FN // 2)
            return w_2raw[:, k, :], w2_h[:, k, :], w2_l[:, k, :]

        def gelu_buffers(f):
            q = f["buffer"]
            return [XV[:, a, q, :, :] if q < 2 else PB_halves[:, a, q - 2, :, :] for a in range(2)]

        def gelu_output(b, half):
            return U_last if (b, half) == (B - 1, 1) else U

        def wait_gelu(e, f):
            e.wait_ge(u_ready[f["ulo"]], f["ulo_count"])

        def write_gelu_lo(e, f):
            b, half, i = f["args"]
            u = [gelu_output(b, half)[:, k, 2 * i:2 * i + 2, :] for k in range(2)]
            e.wait_ge(g_full, f["gelu"] + 1)
            e.tensor_tensor(u[1], gelu_buffers(f)[1], u[0].bitcast(F32), ALU.subtract).then_inc(u_ready[f["ulo"]], 1)

        def split_tile(f):
            if f["kind"] == "qk":
                return [QK[:, f["args"][1], i, :] for i in range(2)]
            if f["kind"] == "turn2":
                return [AH[:, i, :, f["args"][1] * HALF:(f["args"][1] + 1) * HALF] for i in range(2)]
            return [HT[:, i, f["args"][1], :] for i in range(2)]

        def full_tile(f):
            t = FULL[:, f["split"] % 2, :]
            return t.rearrange("p (k n) -> p k n", k=KT) if f["kind"] == "turn2" else t

        def divide(e, x):
            T, cs = x["T"], slice(x["c"] * HALF, (x["c"] + 1) * HALF)
            e.wait_ge(recip, x["n"] + 1)
            e.tensor_tensor(OC[:, T, cs], OC[:, T, cs], LC[:, T, cs], ALU.mult).then_inc(attn_full[x["eng"]], 1)

        def divide_lo(e, x):
            T, cs = x["T"], slice(x["c"] * HALF, (x["c"] + 1) * HALF)
            e.wait_ge(attn_hi, x["n"] + 1)
            e.wait_ge(attn_full[x["eng"]], x["count"])
            e.tensor_tensor(AH[:, 1, T, cs], OC[:, T, cs], AH[:, 0, T, cs].bitcast(F32),
                            ALU.subtract).then_inc(attn_split[x["eng"]], 1)

        def newton(e, link, x):
            ts = slice(x["tiles"][0], x["tiles"][-1] + 1)
            for _ in range(3):
                link(e.tensor_tensor(rt[:, ts], rs[:, ts], rs[:, ts], ALU.mult))
                if x["eng"] == "dve":
                    link(e.scalar_tensor_tensor(out=rt[:, ts], in0=rt[:, ts], scalar=-0.5, in1=ve[:, ts],
                                                op0=ALU.mult, op1=ALU.mult))
                    link(e.scalar_tensor_tensor(out=rs[:, ts], in0=rt[:, ts], scalar=1.5, in1=rs[:, ts],
                                                op0=ALU.add, op1=ALU.mult))
                else:
                    link(e.tensor_tensor(rt[:, ts], rt[:, ts], ve[:, ts], ALU.mult))
                    link(e.tensor_scalar(rt[:, ts], rt[:, ts], -0.5, 1.5, ALU.mult, ALU.add))
                    link(e.tensor_tensor(rs[:, ts], rs[:, ts], rt[:, ts], ALU.mult))
            link(e.tensor_tensor(nmr[:, ts], mv[:, ts, 0], rs[:, ts], ALU.mult))
            link(e.tensor_scalar(nmr[:, ts], nmr[:, ts], -1.0, 0.0, ALU.mult, ALU.add))

        def write_normed(e, x):
            for old in norms[:x["n"]][-2:]:
                turned = ("turn2", old["b"], old["tiles"][-1] // 2) if old["m"] else ("turn1", old["b"], KT - 1)
                if set(old["tiles"]) & set(x["tiles"]):
                    e.wait_ge(filled, find(*turned)["n"] + 1)
            for t in x["tiles"]:
                ins = e.tensor_scalar(NRM[:, t, :], X[:, x["b"] * TT + t, :], rs[:, t:t + 1], nmr[:, t:t + 1],
                                      ALU.mult, ALU.add)
            ins.then_inc(normed[x["eng"]], 1)

        norms = [a[0] for k, a in plan if k == "ln"]
        divisions = [a[0] for k, a in plan if k == "divide"]

        def wait_normed(e, m, b, t):
            x = next(x for x in norms if (x["m"], x["b"]) == (m, b) and t in x["tiles"])
            e.wait_ge(normed[x["eng"]], x["count"])

        def wait_lo(e, f):
            e.wait_ge(split[f["lo"]], f["lo_count"])

        def wait_division(e, sems, upto):
            for eng in sems:
                done = [x["count"] for x in divisions[:upto] if x["eng"] == eng]
                if done:
                    e.wait_ge(sems[eng], done[-1])

        res_order = [(k, a[0]) for k, a in plan if k in ("residual1", "residual2")]
        block = ctx.enter_context(nc.Block())

        @block.sync
        def _(sp):
            for kind, a in plan:
                if kind == "setup":
                    xv = x.rearrange("b (t p) c -> b p t c", p=P)
                    av = w_ada.rearrange("(k p) n -> p k n", p=P)
                    sp.dma_start(X[:, 0:TT, :], xv[0]).then_inc(x_in[0], 16)
                    sp.dma_start(PC[:, :], cols).then_inc(cols_in, 16)
                    sp.dma_start(w_adaraw[:, :, 0:2 * C], av[:, :, 0:2 * C]).then_inc(ada0_in, 16)
                    sp.dma_start(w_qraw, w_qkv.rearrange("(k p) n -> p k n", p=P)).then_inc(wq_in, 16)
                    sp.dma_start(RW[:, :, :].rearrange("p r c -> p (r c)"),
                                 rows.broadcast_to([P, 4 * C])).then_inc(rows_in, 16)
                    sp.wait_ge(consts, 3)
                    for half in range(2):
                        sp.dma_start(KA[64 * half + QROWS:64 * half + QROWS + MROWS, :, :].bitcast(F32),
                                     MR[0:MROWS, :].bitcast(F32).unsqueeze(1).broadcast_to([MROWS, H // 2, N])
                                     ).then_inc(ones_in, 16)
                    sp.dma_start(TR[:, :, :].rearrange("p r c -> p (r c)"),
                                 trows.broadcast_to([P, 5 * C])).then_inc(trows_in, 16)
                    sp.dma_start(w_adaraw[:, :, 2 * C:6 * C], av[:, :, 2 * C:6 * C]).then_inc(ada1_in, 16)
                    for b in range(1, B):
                        sp.dma_start(X[:, b * TT:(b + 1) * TT, :], xv[b]).then_inc(x_in[b], 16)
                    sp.dma_start(w_praw[:, :, :], w_proj.rearrange("(k p) n -> p k n", p=P)).then_inc(wp_in, 16)
                if kind == "load_mlp":
                    sp.wait_ge(filled, find("ada", 1)["n"] + 1)
                    sp.wait_ge(filled, find("gate", B - 1, 1)["n"] + 1)
                    sp.dma_start(w_1raw[:, :, :], w_fc1.rearrange("(k p) n -> p k n", p=P)).then_inc(w1_in, 16)
                    sp.dma_start(w_2raw[:, :, :], w_fc2.rearrange("(k p) n -> p k n", p=P)).then_inc(w2_in, 16)
                if kind == "qk_rows":
                    b, mt = a
                    if b >= 1:
                        sp.wait_ge(scored, GH * ((b - 1) * G * TT + (8 if mt == 0 else 16)))
                    for dst, which, parts in ((QA, 0, (0, 0, 1)), (KA, 1, (0, 1, 0))):
                        wait_lo(sp, find("qk", b, which, mt))
                        for half in range(2):
                            for blk, hl in enumerate(parts):
                                sp.dma_start(
                                    dst[64 * half + D * blk:64 * half + D * (blk + 1), 4 * mt:4 * mt + 4, :].bitcast(F32),
                                    QK[64 * half:64 * half + 64, which, hl, :].bitcast(F32)).then_inc(qk_in[mt], 16)
                if kind == "fill" and a[0]["kind"] == "maxrow":
                    b, g = a[0]["args"]
                    sp.wait_ge(rel["act"], a[0]["count"])
                    for half in range(2):
                        sp.dma_start(QA[64 * half + QROWS:64 * half + QROWS + MROWS, 2 * g:2 * g + 2, :].bitcast(F32),
                                     MR[4 * half:4 * half + 4, :].bitcast(F32)).then_inc(mrow_in[g % 2], 16)
                if kind == "attn_out":
                    n = a[0]
                    b, g = divmod(n, G)
                    sp.wait_ge(o_copied, n + 1)
                    if g in (0, 2) and b >= 1:
                        last_use = (b - 1) * 4 + (4 if g else 2)
                        wait_division(sp, attn_split, last_use)
                        wait_division(sp, attn_full, last_use)
                    part = slice(64 * (g % 2), 64 * (g % 2) + 64)
                    sp.dma_start(OC[part, g // 2, :], OS[0:P:2, :]).then_inc(o_in, 16)
                    sp.dma_start(LC[part, g // 2, :], OS[1:P:2, :]).then_inc(o_in, 16)
                if kind == "fill" and a[0]["kind"] == "fc2":
                    b, t = a[0]["args"]
                    k = b * TT + t
                    sp.wait_ge(y_ready, k + 1)
                    sp.dma_start(out[b, t * P:(t + 1) * P, :], X[:, k, :]).then_inc(y_out, 16)
            sp.wait_ge(y_out, 16 * NT)

        @block.tensor
        def _(pe):
            def products(psum, left, right, tiles, lo, hi):
                parts = ((0, 0), (1, 0), (0, 1))
                mm = None
                for k in range(tiles):
                    for i, (l, r) in enumerate(parts):
                        if lo <= 3 * k + i < hi:
                            mm = pe.matmul(psum, left(l, k), right(r, k), start=(k == 0 and i == 0),
                                           stop=(k == tiles - 1 and i == 2))
                return mm

            for kind, a in plan:
                if kind == "part" or kind == "fill" and not a[0]["parted"]:
                    if kind == "part":
                        what, args, number, lo, hi = a
                        last_part = hi == MATMULS[what]
                    else:
                        what, args, number, lo = a[0]["kind"], a[0]["args"], a[0]["n"], 0
                        hi, last_part = MATMULS.get(what), True
                    if number >= RING and lo == 0:
                        old = fills[number - RING]
                        pe.wait_ge(rel[old["eng"]], old["count"])
                    ps = SM[number % RING]
                    if what == "ada":
                        pe.wait_ge(silu_ready, 1)
                        pe.wait_ge((ada0_in, ada1_in)[args[0]], 16)
                        first = SH_MLP if args[0] else SH_MSA
                        for c in range(2 * KT):
                            for k in range(KT):
                                mm = pe.matmul(ps[:, B * c:B * c + B],
                                               w_adaraw[:, k, first * C + c * P:first * C + (c + 1) * P],
                                               silu[:, k * B:(k + 1) * B], start=(k == 0), stop=(k == KT - 1))
                    elif what == "gate":
                        b, m = args
                        pe.wait_ge(silu_ready, 2)
                        pe.wait_ge(ada1_in, 16)
                        c0 = (G_MLP if m else G_MSA) * C
                        for k in range(KT):
                            mm = pe.matmul(ps[:, 0:C], silu_wide[:, k, b, :], w_adaraw[:, k, c0:c0 + C],
                                           start=(k == 0), stop=(k == KT - 1))
                    elif what in ("turn1", "turn2"):
                        pe.wait_ge(consts, 2)
                        if what == "turn1":
                            parts = [(t, args[1]) for t in range(TT)]
                        else:
                            parts = [(2 * args[1] + t, k) for k in range(KT) for t in range(2)]
                        wait_normed(pe, int(what[-1]) - 1, args[0], parts[0][0])
                        for at, (t, k) in enumerate(parts):
                            mm = pe.transpose(ps[:, at * P:(at + 1) * P], NRM[:, t, k * P:(k + 1) * P], ident[:, :])
                    elif what == "qk":
                        b, which, mt = args
                        pe.wait_ge(wq_split, 1)
                        for k in range(KT):
                            wait_lo(pe, find("turn1", b, k))
                        c0 = which * C + mt * P
                        mm = products(ps[:, :], lambda l, k: (wqkv_h, wqkv_l)[l][:, k, c0:c0 + P],
                                      lambda r, k: HT[:, r, k, :], KT, lo, hi)
                    elif what == "v":
                        b, t = args
                        pe.wait_ge(wq_split, 1)
                        for k in range(KT):
                            wait_lo(pe, find("turn1", b, k))
                        mm = products(ps[:, 0:C], lambda l, k: HT[:, l, k, t * P:(t + 1) * P],
                                      lambda r, k: (wqkv_h, wqkv_l)[r][:, k, 2 * C:3 * C], KT, lo, hi)
                    elif what == "max":
                        b, g, j, t = args
                        h = g * GH + j
                        if (g % 2, j, t) == (0, 0, 0):
                            pe.wait_ge(qk_in[g // 2], 16 * 12 * (b + 1))
                        r = half_rows(h)
                        mm = pe.matmul(ps[:, :], QA[r:r + QROWS, h // 2, t * P:(t + 1) * P],
                                       KA[r:r + QROWS, h // 2, :], start=True, stop=True)
                    elif what == "maxrow":
                        b, g = args
                        pe.wait_ge(maxed, b * G + g + 1)
                        for t in range(TT):
                            mm = pe.transpose(ps[0:2 * GH, t * P:(t + 1) * P], ms[:, t, :].bitcast(F32), ident[:, :])
                    elif what == "proj":
                        b, t = args
                        wait_division(pe, attn_split, 4 * b + 3 + t // 2)
                        pe.wait_ge(w_split, 1)
                        mm = products(ps[:, 0:C], lambda l, k: AH[:, l, k, t * P:(t + 1) * P],
                                      lambda r, k: (wp_h, wp_l)[r][:, k, :], KT, lo, hi)
                    elif what == "fc1":
                        b, half, i = args
                        wait_lo(pe, find("turn2", b, half))
                        pe.wait_ge(w_split, 3)
                        for e in range(lo // (3 * KT), hi // (3 * KT)):
                            c0 = (2 * i + e) * P
                            mm = products(ps[:, e * HALF:(e + 1) * HALF], lambda l, k: (w1_h, w1_l)[l][:, k, c0:c0 + P],
                                          lambda r, k: AH[:, r, k, half * HALF:(half + 1) * HALF],
                                          KT, 0, 3 * KT)
                    elif what == "fc2":
                        b, t = args
                        pe.wait_ge(w_split, 5)
                        for i in range(FN // 2):
                            wait_gelu(pe, find("fc1", b, t // 2, i))
                        c0, u = (t % 2) * P, gelu_output(b, t // 2)
                        mm = products(ps[:, 0:C], lambda l, k: u[:, l, k, c0:c0 + P],
                                      lambda r, k: (w2_h, w2_l)[r][:, k, :], FN, lo, hi)
                    if last_part:
                        mm.then_inc(filled, 1)
                if kind == "scores":
                    s, j = a
                    b, i = divmod(s, G * TT)
                    g, kt = divmod(i, TT)
                    n, unit = s // TT, GH * s + j
                    if unit >= SCORE_RING:
                        pe.wait_ge(exped, unit - SCORE_RING + 1)
                    if kt == 0 and j == 0:
                        pe.wait_ge(mrow_in[g % 2], 32 * (n // 2 + 1))
                        if n == 0:
                            pe.wait_ge(ones_in, 32)
                    h = g * GH + j
                    r = half_rows(h)
                    pe.matmul(ST[unit % SCORE_RING][:, :], KA[r:r + QROWS + MROWS, h // 2, kt * P:(kt + 1) * P],
                              QA[r:r + QROWS + MROWS, h // 2, :], start=True, stop=True).then_inc(scored, 1)
                if kind == "values":
                    s = a[0]
                    b, i = divmod(s, G * TT)
                    g, kt = divmod(i, TT)
                    n = s // TT
                    pe.wait_ge(exped, GH * (s + 1))
                    if i == 0:
                        pe.wait_ge(v_ready, TT * (b + 1))
                    if kt == 0 and n >= 1:
                        pe.wait_ge(o_copied, n)
                    for j in range(GH):
                        mm = pe.matmul(O[2 * D * j:2 * D * (j + 1), :], VA[:, kt, g * GH + j, :],
                                       PB[:, s % 2, j, :], start=(kt == 0), stop=(kt == TT - 1))
                    mm.then_inc(valued, 1)

        @block.scalar
        def _(act):
            for kind, a in plan:
                if kind == "setup":
                    act.wait_ge(cols_in, 16)
                    act.activation(tnh[:, :], col("cond", 0, 2 * B), ACT.Tanh, scale=0.5).then_inc(tanh_c, 1)
                    act.wait_ge(wq_in, 16)
                    act.activation(wqkv_h[:, :, :], w_qraw, ACT.Copy).then_inc(wq_hi, 1)
                if kind == "fill" and a[0]["eng"] == "act":
                    f = a[0]
                    what, args, ps = f["kind"], f["args"], SM[f["slot"]]
                    act.wait_ge(filled, f["n"] + 1)
                    if what in ("turn1", "turn2", "qk"):
                        if f["split"] >= 2:
                            wait_lo(act, next(x for x in fills if x.get("split") == f["split"] - 2))
                        if what == "qk":
                            b, which, mt = args
                            if mt == 1:
                                act.wait_ge(qk_in[0], 16 * 12 * (b + 1))
                            elif b >= 1:
                                act.wait_ge(qk_in[1], 16 * 12 * b)
                            act.wait_ge(silu_ready, 1)
                            i = 2 * which + mt
                            dst, bias, scale = QK[:, which, 0, :], qkb[:, i:i + 1], qkg[:, i:i + 1]
                        elif what == "turn1":
                            b, k = args
                            act.wait_ge(affine, 1)
                            dst = HT[:, 0, k, :]
                            bias, scale = LB[:, 0, k, b:b + 1], LA[:, 0, k, b:b + 1]
                        if what != "turn2":
                            act.activation(full_tile(f), ps[:, :], ACT.Identity, bias=bias, scale=scale)
                            act.activation(dst, ps[:, :], ACT.Identity, bias=bias, scale=scale).then_inc(rel["act"], 1)
                        else:
                            b, c = args
                            act.wait_ge(affine, 2)
                            for dst in (full_tile(f), AH[:, 0, :, c * HALF:(c + 1) * HALF]):
                                for k in range(KT):
                                    ins = act.activation(dst[:, k, :], ps[:, k * HALF:(k + 1) * HALF], ACT.Identity,
                                                         bias=LB[:, 1, k, b:b + 1], scale=LA[:, 1, k, b:b + 1])
                            ins.then_inc(rel["act"], 1)
                    elif what == "maxrow":
                        b, g = args
                        n = b * G + g
                        if n >= 1:
                            act.wait_ge(mrow_in[(g - 1) % 2], 32 * ((n - 1) // 2 + 1))
                        else:
                            act.wait_ge(ones_in, 32)
                        act.activation(MR[:, :], ps[0:2 * GH, :], ACT.Copy).then_inc(rel["act"], 1)
                    elif what == "fc1":
                        b, half, i = args
                        q = f["gelu"]
                        for x in reversed(fills[:f["n"]]):
                            if x.get("buffer") == f["buffer"]:
                                wait_gelu(act, x)
                                break
                        if b == B - 1:
                            act.wait_ge(valued, STEPS)
                        for func, dst in zip((ACT.Identity, ACT.Square), gelu_buffers(f)):
                            for e in range(2):
                                mm = act.activation(dst[:, e, :], ps[:, e * HALF:(e + 1) * HALF], func,
                                                    bias=col("fc1_b", 2 * i + e))
                        mm.then_inc(rel["act"], 1)
                if kind == "gelu_c":
                    q = a[0]["gelu"]
                    act.wait_ge(g_mid, q + 1)
                    vg = gelu_buffers(a[0])[1]
                    act.activation(vg, vg, ACT.Tanh,
                                   scale=GELU_SCALE * GELU_CUBIC).then_inc(g_tanh, 1)
                if kind == "scores":
                    s, j = a
                    unit = GH * s + j
                    act.wait_ge(scored, unit + 1)
                    if s == 1:
                        act.wait_ge(wq_split, 1)
                    if s >= 2:
                        act.wait_ge(valued, s - 1)
                    act.activation(PB[:, s % 2, j, :], ST[unit % SCORE_RING][:, :], ACT.Exp).then_inc(exped, 1)
                if kind == "attn_out":
                    n = a[0]
                    act.wait_ge(valued, TT * (n + 1))
                    if n >= 1:
                        act.wait_ge(o_in, 32 * n)
                    act.activation(OS[:, :], O[:, :], ACT.Copy).then_inc(o_copied, 1)
                if kind == "weights":
                    i = a[0]
                    act.wait_ge((wp_in, w1_in, w1_in, w2_in, w2_in)[i], 16)
                    raw, h, _l = weight_parts(i)
                    act.activation(h, raw, ACT.Copy).then_inc(w_hi, 1)
                if kind == "attn_hi":
                    x = a[0]
                    b, T, cs = x["b"], x["T"], slice(x["c"] * HALF, (x["c"] + 1) * HALF)
                    act.wait_ge(attn_full[x["eng"]], x["count"])
                    if b >= 1:
                        act.wait_ge(filled, find("fc1", b - 1, 1, 3)["n"] + 1)
                    act.activation(AH[:, 0, T, cs], OC[:, T, cs], ACT.Copy).then_inc(attn_hi, 1)

        @block.vector
        def _(dve):
            done = [0]
            seen_aggr = [0]

            def link(ins):
                done[0] += 1
                ins.then_inc(dve_seq, 1)
                dve.wait_ge(dve_seq, done[0])

            def take(f):
                dve.wait_ge(filled, f["n"] + 1)
                return SM[f["slot"]]

            for kind, a in plan:
                if kind == "setup":
                    dve.wait_ge(cols_in, 16)
                    dve.wait_ge(tanh_c, 1)
                    link(dve.scalar_tensor_tensor(out=silu[:, :], in0=tnh[:, :], scalar=1.0,
                                                  in1=col("cond", 0, 2 * B), op0=ALU.add, op1=ALU.mult))
                    dve.tensor_scalar(qkg[:, 0:2], col("qk_g", 0, 2), float(D) ** -0.5, None, ALU.mult)
                    dve.tensor_copy(qkg[:, 2:4], col("qk_g", 2, 2))
                    dve.tensor_scalar(adab1[:, :], col("ada_b", 0, 12), 1.0, None, ALU.add)
                    link(dve.tensor_scalar(silu[:, :], silu[:, :], 0.5, None, ALU.mult))
                    dve.tensor_tensor(qkb[:, :], col("qk_b", 0, 4), qkg[:, :], ALU.mult).then_inc(silu_ready, 1)
                if kind == "fill" and a[0]["eng"] == "dve":
                    f = a[0]
                    what, args = f["kind"], f["args"]
                    ps = take(f)
                    if what == "ada":
                        m = args[0]
                        sh, sc = ((SH_MSA, SC_MSA), (SH_MLP, SC_MLP))[m]
                        w, bb = ("ln1_w", "ln1_b") if m == 0 else ("ln2_w", "ln2_b")
                        p_sh = [ps[:, B * k:B * k + B] for k in range(KT)]
                        p_sc = [ps[:, B * (KT + k):B * (KT + k) + B] for k in range(KT)]
                        for k in range(KT):
                            one = adab1[:, sc * KT + k:sc * KT + k + 1]
                            dve.tensor_scalar(LA[:, m, k, :], p_sc[k], one, col(w, k), ALU.add, ALU.mult)
                            ins = dve.tensor_scalar(lt[:, k, :], p_sc[k], one, col(bb, k), ALU.add, ALU.mult)
                        link(ins)
                        for k in range(KT):
                            ins = dve.scalar_tensor_tensor(out=LB[:, m, k, :], in0=p_sh[k],
                                                           scalar=col("ada_b", sh * KT + k), in1=lt[:, k, :],
                                                           op0=ALU.add, op1=ALU.add)
                        ins.then_inc(affine, 1)
                        dve.wait_ge(affine, m + 1)
                        dve.tensor_copy(lt[:, :, :], LA[:, m, :, :]).then_inc(rel["dve"], 1)
                    elif what == "gate":
                        b, m = args
                        dve.wait_ge(trows_in, 16)
                        dve.tensor_tensor(GATE[:, b, m, :], ps[:, 0:C], TR[:, TROW_AMLP if m else TROW_AMSA, :],
                                          ALU.add).then_inc(rel["dve"], 1)
                    elif what == "v":
                        b, t = args
                        k = b * TT + t
                        dve.wait_ge(rows_in, 16)
                        if b >= 1:
                            dve.wait_ge(v_ready, TT * b)
                        dve.tensor_tensor(VT[:, t, :], ps[:, 0:C], RW[:, ROW_BV, :], ALU.add).then_inc(rel["dve"], 1)
                    elif what == "max":
                        b, g, j, t = args
                        n = b * G + g
                        if (j, t) == (0, 0) and n >= 1:
                            dve.wait_ge(maxed, n)
                        pos = 2 * (j % 2) + j // 2
                        dve.tensor_reduce(nm[:, t, pos:pos + 1], ps[:, :], AX.X, ALU.max,
                                          negate=True).then_inc(rel["dve"], 1)
                        if (j, t) == (GH - 1, TT - 1):
                            dve.wait_ge(rel["dve"], f["count"])
                            if n >= 1:
                                dve.wait_ge(filled, find("maxrow", *divmod(n - 1, G))["n"] + 1)
                            nmv = nm[:, :, :].rearrange("p t (a l) -> p t a l", a=2)
                            msv = ms[:, :, :].rearrange("p t (a s l) -> p t a s l", a=2, s=2)
                            for half in range(2):
                                ins = dve.tensor_copy(msv[:, :, half, 0, :], nmv[:, :, half, :])
                            link(ins)
                            for half in range(2):
                                ins = dve.tensor_tensor(msv[:, :, half, 1, :], nmv[:, :, half, :],
                                                        msv[:, :, half, 0, :].bitcast(F32), ALU.subtract)
                            ins.then_inc(maxed, 1)
                    elif what == "proj":
                        b, t = args
                        dve.wait_ge(gate_ready, 2 * B)
                        dve.wait_ge(biased, res_order.index(("residual1", b)) + 1)
                        xt = X[:, b * TT + t, :]
                        if t >= 1:
                            dve.wait_ge(x2_ready, b * TT + t)
                        elif b >= 1:
                            dve.wait_ge(y_ready, b * TT)
                        dve.tensor_tensor(PT[:, :], ps[:, 0:C], GATE[:, b, 0, :], ALU.mult).then_inc(rel["dve"], 1)
                        dve.wait_ge(rel["dve"], f["count"])
                        dve.tensor_tensor(xt, PT[:, :], xt, ALU.add).then_inc(x2_ready, 1)
                    elif what == "fc2":
                        b, t = args
                        k = b * TT + t
                        dve.wait_ge(biased, res_order.index(("residual2", b)) + 1)
                        if t == 0:
                            dve.wait_ge(x2_ready, (b + 1) * TT)
                        else:
                            dve.wait_ge(y_ready, k)
                        dve.tensor_tensor(PT[:, :], ps[:, 0:C], GATE[:, b, 1, :], ALU.mult).then_inc(rel["dve"], 1)
                        dve.wait_ge(rel["dve"], f["count"])
                        dve.tensor_tensor(X[:, k, :], PT[:, :], X[:, k, :], ALU.add).then_inc(y_ready, 1)
                if kind == "gelu_b":
                    f = a[0]
                    q = f["gelu"]
                    dve.wait_ge(rel["act"], f["count"])
                    xg, vg = gelu_buffers(f)
                    dve.scalar_tensor_tensor(out=vg, in0=vg, scalar=1.0 / GELU_CUBIC, in1=xg,
                                             op0=ALU.add, op1=ALU.mult).then_inc(g_mid, 1)
                if kind == "gelu_d":
                    f = a[0]
                    q = f["gelu"]
                    b, half, i = f["args"]
                    xg, vg = gelu_buffers(f)
                    dve.wait_ge(g_tanh, q + 1)
                    link(dve.scalar_tensor_tensor(out=vg, in0=vg, scalar=1.0, in1=xg, op0=ALU.add, op1=ALU.mult))
                    if (b, half) == (B - 1, 1):
                        dve.wait_ge(scored, GH * STEPS)
                    elif i == 0 and (b, half) != (0, 0):
                        b0, h0 = (b, 0) if half else (b - 1, 1)
                        dve.wait_ge(filled, find("fc2", b0, 2 * h0 + 1)["n"] + 1)
                    if q == 0:
                        dve.wait_ge(w_split, 5)
                        dve.wait_ge(w_hi, 5)
                    dve.tensor_copy(gelu_output(b, half)[:, 0, 2 * i:2 * i + 2, :], vg).then_inc(g_full, 1)
                if kind == "gelu_lo" and a[0]["ulo"] == "dve":
                    write_gelu_lo(dve, a[0])
                if kind == "silu_wide":
                    dve.wait_ge(consts, 2)
                    for k in range(KT):
                        for b in range(B):
                            mm = dve.tensor_scalar(silu_wide[:, k, b, :], ident[:, :], 0.0,
                                                   silu[:, k * B + b:k * B + b + 1], ALU.mult, ALU.add)
                    mm.then_inc(silu_ready, 1)
                if kind == "wq_lo":
                    dve.wait_ge(wq_hi, 1)
                    dve.wait_ge(wq_in, 16)
                    dve.tensor_tensor(wqkv_l[:, :, :], w_qraw, wqkv_h[:, :, :].bitcast(F32),
                                      ALU.subtract).then_inc(wq_split, 1)
                if kind == "lo":
                    f = a[0]
                    dve.wait_ge(rel["act"], f["count"])
                    h, l = split_tile(f)
                    dve.tensor_tensor(l, full_tile(f), h.bitcast(F32),
                                      ALU.subtract).then_inc(split["dve"], 1)
                if kind == "stats":
                    m, b, t = a
                    if m == 0:
                        dve.wait_ge(x_in[b], 16)
                    else:
                        dve.wait_ge(x2_ready, TT * b + t + 1)
                    if seen_aggr[0]:
                        dve.wait_ge(aggregated, seen_aggr[0])
                    dve.bn_stats(st6[:, t, :], X[:, b * TT + t, :]).then_inc(stats_done, 1)
                if kind == "ln":
                    x = a[0]
                    dve.wait_ge(stats_done, x["stats"])
                    ts = slice(x["tiles"][0], x["tiles"][-1] + 1)
                    for e in range(x["n"]):
                        if e == x["n"] - 1:
                            dve.wait_ge(normed[norms[e]["eng"]], norms[e]["count"])
                    for t in x["tiles"]:
                        ins = dve.bn_aggr(mv[:, t, :], st6[:, t, :])
                    ins.then_inc(aggregated, 1)
                    seen_aggr[0] += 1
                    dve.wait_ge(aggregated, seen_aggr[0])
                    link(dve.tensor_scalar(ve[:, ts], mv[:, ts, 1], EPS, None, ALU.add))
                    ins = dve.tensor_scalar(rs[:, ts].bitcast(I32), ve[:, ts].bitcast(I32), -0.5, RSQRT_SEED,
                                            ALU.mult, ALU.add)
                    if x["eng"] == "pool":
                        ins.then_inc(seeded, 1)
                    else:
                        link(ins)
                        newton(dve, link, x)
                        write_normed(dve, x)
                if kind == "recip":
                    b, T, c = a
                    dve.wait_ge(o_in, 32 * (G * b + 2 * T + 2))
                    cs = slice(c * HALF, (c + 1) * HALF)
                    dve.reciprocal(LC[:, T, cs], LC[:, T, cs]).then_inc(recip, 1)
                if kind == "divide" and a[0]["eng"] == "dve":
                    divide(dve, a[0])
                if kind == "attn_lo" and a[0]["eng"] == "dve":
                    divide_lo(dve, a[0])

        @block.gpsimd
        def _(pool):
            seq = [0]

            def link(ins):
                seq[0] += 1
                ins.then_inc(pool_seq, 1)
                pool.wait_ge(pool_seq, seq[0])

            def lo(dst, full, hi):
                return pool.tensor_tensor(dst, full, hi.bitcast(F32), ALU.subtract)

            for kind, a in plan:
                if kind == "setup":
                    pool.memset(ident[:, :], 0.0).then_inc(consts, 1)
                    pool.wait_ge(consts, 1)
                    pool.affine_select(out=ident[:, :], in_=ident[:, :], compare_op=ALU.not_equal, fill=1.0,
                                       base=0, pattern=[[-1, P]], channel_multiplier=1).then_inc(consts, 1)
                    pool.memset(MR[:, :].bitcast(F32), 1.0).then_inc(consts, 1)
                    pool.memset(VA[:, :, :, :], 1.0).then_inc(pool_seq, 1)
                    seq[0] += 1
                    pool.wait_ge(pool_seq, seq[0])
                if kind == "ln" and a[0]["eng"] == "pool":
                    pool.wait_ge(seeded, a[0]["count"])
                    newton(pool, link, a[0])
                    write_normed(pool, a[0])
                if kind == "residual1" or kind == "residual2":
                    b, m = a[0], int(kind[-1]) - 1
                    wait_normed(pool, m, b, TT - 1)
                    pool.wait_ge(gate_ready, 2 * b + m + 1)
                    at = res_order.index((kind, b))
                    if at >= 1:
                        pool.wait_ge(biased, at)
                    link(pool.tensor_tensor(GB[:, :], GATE[:, b, m, :], RW[:, ROW_B2 if m else ROW_BP, :], ALU.mult))
                    for t in range(TT):
                        ins = pool.tensor_tensor(X[:, b * TT + t, :], X[:, b * TT + t, :], GB[:, :], ALU.add)
                    ins.then_inc(biased, 1)
                if kind == "weights":
                    pool.wait_ge(w_hi, a[0] + 1)
                    raw, h, l = weight_parts(a[0])
                    lo(l, raw, h).then_inc(w_split, 1)
                if kind == "fill":
                    f = a[0]
                    what, args = f["kind"], f["args"]
                    if f.get("lo") == "pool":
                        pool.wait_ge(rel["act"], f["count"])
                        h, l = split_tile(f)
                        lo(l, full_tile(f), h).then_inc(split["pool"], 1)
                    if what == "gate":
                        b, m = args
                        if (b, m) == (0, 0):
                            pool.wait_ge(trows_in, 16)
                            pool.wait_ge(rows_in, 16)
                            link(pool.tensor_tensor(TR[:, TROW_G1, :], TR[:, TROW_G1, :], TR[:, TROW_GO, :], ALU.mult))
                            link(pool.tensor_scalar(TR[:, TROW_G2, :], TR[:, TROW_G2, :], 0.5, 1.0, ALU.mult, ALU.mult))
                            link(pool.tensor_scalar(RW[:, ROW_B2, :], RW[:, ROW_B2, :], 2.0, 1.0, ALU.mult, ALU.mult))
                        pool.wait_ge(rel["dve"], f["count"])
                        pool.tensor_tensor(GATE[:, b, m, :], GATE[:, b, m, :], TR[:, TROW_G2 if m else TROW_G1, :],
                                           ALU.mult).then_inc(gate_ready, 1)
                if kind == "v_place":
                    b = a[0]
                    pool.wait_ge(rows_in, 16)
                    if b >= 1:
                        pool.wait_ge(valued, G * TT * b)
                    for t in range(TT):
                        pool.wait_ge(rel["dve"], find("v", b, t)["count"])
                        pool.tensor_tensor(VA[:, t, :, 0:2 * D:2],
                                           VT[:, t, :].rearrange("p (h d) -> p h d", h=H),
                                           RW[:, ROW_GV, :].rearrange("p (h d) -> p h d", h=H),
                                           ALU.mult).then_inc(v_ready, 1)
                if kind == "gelu_lo" and a[0]["ulo"] == "pool":
                    write_gelu_lo(pool, a[0])
                if kind == "divide" and a[0]["eng"] == "pool":
                    divide(pool, a[0])
                if kind == "attn_lo" and a[0]["eng"] == "pool":
                    divide_lo(pool, a[0])


def kernel(x, cond_1024, L0_cond_ln1_w, L0_cond_ln1_b, L0_cond_ln2_w, L0_cond_ln2_b, L0_cond_gamma_qkv,
           L0_cond_gamma_attn_out, L0_cond_w_qkv, L0_cond_b_qkv, L0_cond_w_proj, L0_cond_b_proj, L0_cond_w_fc1,
           L0_cond_b_fc1, L0_cond_w_fc2, L0_cond_b_fc2, L0_cond_w_ada, L0_cond_b_ada, L0_cond_gamma1,
           L0_cond_gamma2):
    import numpy as np
    import concourse.bacc as bacc
    from concourse.bass_utils import run_bass_kernel_spmd as run

    def spread(w):
        w = np.asarray(w)
        lead = w.shape[:-1]
        w = w.reshape(*lead, KT, 4, 2, D)
        return np.moveaxis(w, -3, -1).reshape(*lead, C)

    def tiles(v):
        return np.asarray(v).reshape(-1, P).T

    w_qkv, b_qkv, g_qkv = (np.asarray(v) for v in (L0_cond_w_qkv, L0_cond_b_qkv, L0_cond_gamma_qkv))
    w = np.concatenate([spread(w_qkv[:, 0:C]), spread(w_qkv[:, C:2 * C]), w_qkv[:, 2 * C:]], axis=1)
    qk = [np.concatenate([spread(v[0:C]), spread(v[C:2 * C])]) for v in (b_qkv, g_qkv)]
    cond = np.asarray(cond_1024).reshape(B, KT, P).transpose(2, 1, 0).reshape(P, KT * B)
    cols = np.concatenate([tiles(qk[0]), tiles(qk[1]), tiles(L0_cond_ln1_w), tiles(L0_cond_ln1_b),
                           tiles(L0_cond_ln2_w), tiles(L0_cond_ln2_b), tiles(L0_cond_b_fc1),
                           tiles(L0_cond_b_ada), cond], axis=1)
    b_ada = np.asarray(L0_cond_b_ada).reshape(6, C)
    rows = np.concatenate([b_qkv[2 * C:], g_qkv[2 * C:], np.asarray(L0_cond_b_proj), np.asarray(L0_cond_b_fc2)])
    trows = np.concatenate([np.asarray(L0_cond_gamma1), np.asarray(L0_cond_gamma_attn_out),
                            np.asarray(L0_cond_gamma2), b_ada[G_MSA], b_ada[G_MLP]])
    w_ada = np.asarray(L0_cond_w_ada)
    arrays = {"x": np.asarray(x), "cols": cols, "rows": rows[None, :], "trows": trows[None, :], "w_qkv": w,
              "w_proj": np.asarray(L0_cond_w_proj), "w_fc1": np.asarray(L0_cond_w_fc1),
              "w_fc2": np.asarray(L0_cond_w_fc2), "w_ada": w_ada}
    nc = bacc.Bacc("TRN2", target_bir_lowering=False, num_devices=1)
    arrays = {k: np.ascontiguousarray(v) for k, v in arrays.items()}
    ins = {k: nc.dram_tensor("in_" + k, v.shape, F32, kind="ExternalInput").ap() for k, v in arrays.items()}
    y = nc.dram_tensor("y", (B, N, C), F32, kind="ExternalOutput").ap()
    block_program(nc, out=y, **ins)
    r = run(nc, [{"in_" + k: v for k, v in arrays.items()}], core_ids=[0])
    return r.results[0]["y"]
```
